# Optimizing a Trainium2 kernel written in Bass

```python
import numpy as np
import jax
import jax.numpy as jnp

def _softmax(x, axis=-1):
    return jax.nn.softmax(x, axis=axis)

def _gelu(x):
    return jax.nn.gelu(x, approximate=True)

def _silu(x):
    return jax.nn.silu(x)

def _sigmoid(x):
    return jax.nn.sigmoid(x)

def _layernorm(x, axis=-1, eps=1e-05):
    m = jnp.mean(x, axis=axis, keepdims=True)
    v = jnp.var(x, axis=axis, keepdims=True)
    return (x - m) / jnp.sqrt(v + eps)

def _scatter_add(tgt, idx, src, axis=0):
    return tgt.at[idx].add(src)

def _segment_sum(src, seg, n):
    return jax.ops.segment_sum(src, seg, n)
kernel_name = 'mk_macaron_d2_jaxref_r8_792da3'

def setup_inputs(seed: int=0):
    np.random.seed(seed)
    _w = jnp.asarray

    def _L0_attn_setup():
        import jax, jax.numpy as jnp
        import numpy as np
        B, T, D = (2, 256, 128)
        N_HEADS = 16
        HEAD_DIM = D // N_HEADS
        key = jax.random.key(seed)
        ks = jax.random.split(key, 5)
        s = 0.02
        return {'x': jax.random.normal(ks[0], (B, T, D), jnp.float32), 'wq': jax.random.normal(ks[1], (D, D), jnp.float32) * s, 'wk': jax.random.normal(ks[2], (D, D), jnp.float32) * s, 'wv': jax.random.normal(ks[3], (D, D), jnp.float32) * s, 'wo': jax.random.normal(ks[4], (D, D), jnp.float32) * s, 'bo': jnp.zeros((D,), jnp.float32)}
    _L0_attn_in = _L0_attn_setup()

    def _L0_ffn_setup():
        import jax, jax.numpy as jnp
        import numpy as np
        LN_EPS = 1e-12
        key = jax.random.key(seed)
        ks = jax.random.split(key, 8)
        B, S, H, I, E = (4, 256, 128, 512, 8)
        sH = 1.0 / np.sqrt(H)
        sI = 1.0 / np.sqrt(I)
        return {'hidden_states': jax.random.normal(ks[0], (B, S, H), dtype=jnp.float32), 'Wr': jax.random.uniform(ks[1], (E, H), jnp.float32, -sH, sH), 'W1': jax.random.uniform(ks[2], (E, H, I), jnp.float32, -sH, sH), 'b1': jax.random.uniform(ks[3], (E, I), jnp.float32, -sH, sH), 'Wo': jax.random.uniform(ks[4], (I, H), jnp.float32, -sI, sI), 'bo': jax.random.uniform(ks[5], (H,), jnp.float32, -sI, sI), 'gamma': jnp.ones((H,), jnp.float32), 'beta': jnp.zeros((H,), jnp.float32)}
    _L0_ffn_in = _L0_ffn_setup()

    def _L1_attn_setup():
        import jax, jax.numpy as jnp
        import numpy as np
        import math
        N_EMBD = 128
        N_HEAD = 16
        N_LAYER = 12
        key = jax.random.key(seed)
        kx, kw, kb = jax.random.split(key, 3)
        B, T, C = (4, 256, N_EMBD)
        x = jax.random.normal(kx, (B, T, C), dtype=jnp.float32)
        bound = 1.0 / math.sqrt(C)
        W = jax.random.uniform(kw, (3 * C, C), minval=-bound, maxval=bound, dtype=jnp.float32)
        W = W * (1.0 / math.sqrt(N_LAYER * 2))
        b = jax.random.uniform(kb, (3 * C,), minval=-bound, maxval=bound, dtype=jnp.float32)
        return {'x': x, 'W': W, 'b': b}
    _L1_attn_in = _L1_attn_setup()

    def _L1_ffn_setup():
        import jax, jax.numpy as jnp
        import numpy as np
        EPS = 1e-05

        def _quantize(W):
            gamma = jnp.mean(jnp.abs(W))
            return jnp.clip(jnp.round(W / (gamma + EPS)), -1.0, 1.0)
        key = jax.random.key(seed)
        k_x, k_w1, k_b1, k_w2, k_b2 = jax.random.split(key, 5)
        n_embd = 128
        d_ff = 4 * n_embd
        B, S = (4, 512)
        bound1 = 1.0 / np.sqrt(n_embd)
        bound2 = 1.0 / np.sqrt(d_ff)
        x = jax.random.normal(k_x, (B, S, n_embd), dtype=jnp.float32)
        W1 = jax.random.uniform(k_w1, (d_ff, n_embd), jnp.float32, -bound1, bound1)
        b1 = jax.random.uniform(k_b1, (d_ff,), jnp.float32, -bound1, bound1)
        W2 = jax.random.uniform(k_w2, (n_embd, d_ff), jnp.float32, -bound2, bound2)
        b2 = jax.random.uniform(k_b2, (n_embd,), jnp.float32, -bound2, bound2)
        return {'x': x, 'W1': W1, 'b1': b1, 'W2': W2, 'b2': b2}
    _L1_ffn_in = _L1_ffn_setup()
    _d = {'L0_attn_x': _L0_attn_in['x'], 'L0_attn_wq': _L0_attn_in['wq'], 'L0_attn_wk': _L0_attn_in['wk'], 'L0_attn_wv': _L0_attn_in['wv'], 'L0_attn_wo': _L0_attn_in['wo'], 'L0_attn_bo': _L0_attn_in['bo'], 'L0_ffn_Wr': _L0_ffn_in['Wr'], 'L0_ffn_W1': _L0_ffn_in['W1'], 'L0_ffn_b1': _L0_ffn_in['b1'], 'L0_ffn_Wo': _L0_ffn_in['Wo'], 'L0_ffn_bo': _L0_ffn_in['bo'], 'L0_ffn_gamma': _L0_ffn_in['gamma'], 'L0_ffn_beta': _L0_ffn_in['beta'], 'L1_attn_W': _L1_attn_in['W'], 'L1_attn_b': _L1_attn_in['b'], 'L1_ffn_W1': _L1_ffn_in['W1'], 'L1_ffn_b1': _L1_ffn_in['b1'], 'L1_ffn_W2': _L1_ffn_in['W2'], 'L1_ffn_b2': _L1_ffn_in['b2']}
    _x0 = _d['L0_attn_x']
    _d['L0_attn_x'] = jax.random.normal(jax.random.fold_in(jax.random.key(seed), 1), (1, 2048, 128), dtype=_x0.dtype)
    del _x0
    return _d

def reference(L0_attn_x, L0_attn_wq, L0_attn_wk, L0_attn_wv, L0_attn_wo, L0_attn_bo, L0_ffn_Wr, L0_ffn_W1, L0_ffn_b1, L0_ffn_Wo, L0_ffn_bo, L0_ffn_gamma, L0_ffn_beta, L1_attn_W, L1_attn_b, L1_ffn_W1, L1_ffn_b1, L1_ffn_W2, L1_ffn_b2):

    def _L0_attn_ref(x, wq, wk, wv, wo, bo):
        import jax, jax.numpy as jnp
        import numpy as np
        B, T, D = (2, 256, 128)
        N_HEADS = 16
        HEAD_DIM = D // N_HEADS
        b, t, _ = x.shape

        def split_heads(y):
            return y.reshape(b, t, N_HEADS, HEAD_DIM).transpose(0, 2, 1, 3)
        q = split_heads(x @ wq)
        k = split_heads(x @ wk)
        v = split_heads(x @ wv)
        scores = jnp.einsum('bhqd,bhkd->bhqk', q, k)
        causal = jnp.tril(jnp.ones((t, t), bool))
        scores = jnp.where(causal, scores, -jnp.inf)
        attn = jax.nn.softmax(scores / np.sqrt(HEAD_DIM).astype(np.float32), axis=-1)
        ctx = jnp.einsum('bhqk,bhkd->bhqd', attn, v)
        ctx = ctx.transpose(0, 2, 1, 3).reshape(b, t, D)
        return ctx @ wo + bo

    def _L0_ffn_ref(hidden_states, Wr, W1, b1, Wo, bo, gamma, beta):
        import jax, jax.numpy as jnp
        import numpy as np
        LN_EPS = 1e-12
        B, S, H = hidden_states.shape
        E = Wr.shape[0]
        x = hidden_states.reshape(-1, H)
        router_logits = x @ Wr.T
        expert_idx = jnp.argmax(jax.nn.softmax(router_logits, axis=-1), axis=-1)
        inter = jnp.zeros((x.shape[0], W1.shape[2]), dtype=x.dtype)
        for e in range(E):
            mask = (expert_idx == e)[:, None].astype(x.dtype)
            inter = inter + mask * jax.nn.gelu(x @ W1[e] + b1[e], approximate=False)
        y = inter @ Wo + bo + x
        mu = jnp.mean(y, axis=-1, keepdims=True)
        var = jnp.mean(jnp.square(y - mu), axis=-1, keepdims=True)
        out = (y - mu) * jax.lax.rsqrt(var + LN_EPS) * gamma + beta
        return out.reshape(B, S, H)

    def _L1_attn_ref(x, W, b):
        import jax, jax.numpy as jnp
        import numpy as np
        import math
        N_EMBD = 128
        N_HEAD = 16
        N_LAYER = 12
        B, T, C = x.shape
        H = N_HEAD
        D = C // H
        qkv = jnp.einsum('btc,oc->bto', x, W) + b
        q, k, v = jnp.split(qkv, 3, axis=-1)
        q = q.reshape(B, T, H, D).transpose(0, 2, 1, 3)
        k = k.reshape(B, T, H, D).transpose(0, 2, 1, 3)
        v = v.reshape(B, T, H, D).transpose(0, 2, 1, 3)
        att = jnp.einsum('bhtd,bhsd->bhts', q, k) / math.sqrt(D)
        causal = jnp.tril(jnp.ones((T, T), dtype=bool))
        att = jnp.where(causal, att, -jnp.inf)
        att = jax.nn.softmax(att, axis=-1)
        y = jnp.einsum('bhts,bhsd->bhtd', att, v)
        return y.transpose(0, 2, 1, 3).reshape(B, T, C)

    def _L1_ffn_ref(x, W1, b1, W2, b2):
        import jax, jax.numpy as jnp
        import numpy as np
        EPS = 1e-05

        def _quantize(W):
            gamma = jnp.mean(jnp.abs(W))
            return jnp.clip(jnp.round(W / (gamma + EPS)), -1.0, 1.0)
        Wq1 = _quantize(W1)
        Wq2 = _quantize(W2)
        h = jax.nn.relu(jnp.einsum('bsd,fd->bsf', x, Wq1) + b1)
        out = jnp.einsum('bsf,df->bsd', h, Wq2) + b2
        return out
    x = L0_attn_x
    x = x + 0.5 * _L0_ffn_ref(_layernorm(x, axis=-1), L0_ffn_Wr, L0_ffn_W1, L0_ffn_b1, L0_ffn_Wo, L0_ffn_bo, L0_ffn_gamma, L0_ffn_beta)
    x = x + _L0_attn_ref(_layernorm(x, axis=-1), L0_attn_wq, L0_attn_wk, L0_attn_wv, L0_attn_wo, L0_attn_bo)
    x = x + 0.5 * _L0_ffn_ref(_layernorm(x, axis=-1), L0_ffn_Wr, L0_ffn_W1, L0_ffn_b1, L0_ffn_Wo, L0_ffn_bo, L0_ffn_gamma, L0_ffn_beta)
    x = x + 0.5 * _L1_ffn_ref(_layernorm(x, axis=-1), L1_ffn_W1, L1_ffn_b1, L1_ffn_W2, L1_ffn_b2)
    x = x + _L1_attn_ref(_layernorm(x, axis=-1), L1_attn_W, L1_attn_b)
    x = x + 0.5 * _L1_ffn_ref(_layernorm(x, axis=-1), L1_ffn_W1, L1_ffn_b1, L1_ffn_W2, L1_ffn_b2)
    return x

_drawn_inputs = setup_inputs


def setup_inputs(seed=0):
    import zlib

    import numpy as np

    out = dict(_drawn_inputs(seed))
    spreads = {'L0_attn_bo': (0.0, 0.1), 'L0_ffn_gamma': (1.0, 0.2), 'L0_ffn_beta': (0.0, 0.1)}
    factors = {'L0_attn_wq': 8.0,
     'L0_attn_wk': 8.0,
     'L0_attn_wv': 8.0,
     'L0_attn_wo': 8.0,
     'L0_ffn_b1': 5.837,
     'L0_ffn_bo': 3.652,
     'L1_attn_W': 64.0,
     'L1_attn_b': 64.0,
     'L1_ffn_b1': 8.0,
     'L1_ffn_b2': 192.801}
    for name, (base, spread) in spreads.items():
        noise = np.random.default_rng([zlib.crc32(name.encode()), seed]).standard_normal(out[name].shape)
        drawn = base * np.exp(spread * noise) if base else spread * noise
        out[name] = jnp.asarray(drawn.astype(out[name].dtype))
    for name, factor in factors.items():
        out[name] = (out[name] * factor).astype(out[name].dtype)
    return out
```

```python
from contextlib import ExitStack

import concourse.bass as bass
from concourse import mybir

F32 = mybir.dt.float32
BF16 = mybir.dt.bfloat16
I32 = mybir.dt.int32
ALU = mybir.AluOpType
ACT = mybir.ActivationFunctionType
AX = mybir.AxisListType

P = 128
T = 2048
D = 128
NB = T // P
CH = 512
NCH = T // CH
BPC = CH // P
H = 16
DH = D // H
G = 4
NG = H // G
PAIRS = H // 2
SCALE = float(DH) ** -0.5
E = 8
HID = 512
HT = HID // P
NEG = -1.0e30
NPART = 3
TERMS = (3, 2, 1)
QK_ROWS = DH * sum(TERMS)
KROWS = QK_ROWS + NPART
SLOT = 64
VW = 32


class Chain:

    def __init__(self, semaphore):
        self.semaphore, self.count = semaphore, 0

    def on(self, engine):
        self.engine = engine
        return self

    def __call__(self, instruction):
        instruction.then_inc(self.semaphore, 1)
        self.count += 1
        return instruction

    def wait(self):
        if self.count:
            self.engine.wait_ge(self.semaphore, self.count)


def macaron_layers(nc, x_in, wq, wk, wv, wo, bo, wr, w1, b1, wo2, bo2, gamma, beta,
                   aw, ab, fw1, fb1, fw2, fb2, out):
    stack = ExitStack()
    names = [0]

    def sb(name, shape, dt=F32, where=None):
        names[0] += 1
        return (where or stack).enter_context(nc.sbuf_tensor(f"{name}_{names[0]}", shape, dt))

    def sem(name):
        names[0] += 1
        return stack.enter_context(nc.semaphore(f"{name}_{names[0]}"))

    with stack:
        psum = stack.enter_context(nc.psum_tensor("psum", [P, 8, CH], F32))

        x_res = sb("x_res", [P, NB, D])
        ident = sb("ident", [P, P])
        ident_bf = sb("ident_bf", [P, P], BF16)
        causal_add = sb("causal_add", [P, CH])
        later_keys = sb("later_keys", [P, P], BF16)
        ones_mat = sb("ones_mat", [P, P])
        q_slots = sb("q_slots", [P, PAIRS, T], BF16)
        k_slots = sb("k_slots", [P, PAIRS, T], BF16)
        v_aug = sb("v_aug", [P, NB, H, VW])
        w_qkv0 = sb("w_qkv0", [P, 3, D])
        w_qkv1 = sb("w_qkv1", [P, 3, D])
        wo_sb = sb("wo_sb", [P, D])
        bo_bc = sb("bo_bc", [P, D])
        bv_bc = sb("bv_bc", [P, D])
        bias_cols = sb("bias_cols", [P, 2 + HT])
        qk_bias, fb1_col = bias_cols[:, 0:2], bias_cols[:, 2:2 + HT]
        wr_t = sb("wr_t", [P, E])
        w1_sb = sb("w1_sb", [P, E, HID])
        b1_parts = sb("b1_parts", [NPART * E, HID], BF16)
        wo2_sb = sb("wo2_sb", [P, HT, D])
        bo2_bc = sb("bo2_bc", [P, D])
        gamma_half = sb("gamma_half", [P, D])
        beta_half = sb("beta_half", [P, D])
        rank = sb("rank", [P, E])
        tw1_t = sb("tw1_t", [P, HT, P])
        tw2_t = sb("tw2_t", [P, HT, D])
        fb2_half = sb("fb2_half", [P, D])

        dve_chain = Chain(sem("dve_own"))
        part_dram = [[nc.dram_tensor(f"{n}_part{r}", [D, T], BF16, kind="Internal").ap()
                      for r in range(NPART)] for n in ("q", "k")]
        negmax_dram = nc.dram_tensor("negmax", [NG * NCH, NPART, G * BPC, P], BF16, kind="Internal").ap()

        x_dram = x_in[0].rearrange("(b p) d -> p b d", p=P)
        out_dram = out[0].rearrange("(b p) d -> p b d", p=P)

        def setup():
            local = ExitStack()
            with local:
                wr_in = sb("wr_in", [E, D], where=local)
                aw_in = sb("aw_in", [P, 3, D], where=local)
                fw1_in = sb("fw1_in", [P, HT, D], where=local)
                fw2_in = sb("fw2_in", [P, HID], where=local)
                b1_in = sb("b1_in", [E, HID], where=local)
                b1_rest = sb("b1_rest", [E, HID], where=local)
                b1_rest2 = sb("b1_rest2", [E, HID], where=local)
                b1_split = sb("b1_split", [E, NPART, HID], BF16, where=local)
                abs_sum = sb("abs_sum", [P, 2], where=local)
                half_gamma = sb("half_gamma", [P, 2, 2], where=local)
                below = sb("below", [P, 2, HID], where=local)
                tern = sb("tern", [P, 2, HID], where=local)
                gam_in = sb("gam_in", [P, D], where=local)
                bet_in = sb("bet_in", [P, D], where=local)
                fb2_in = sb("fb2_in", [P, D], where=local)
                col_in = sb("col_in", [2 + HT, D], where=local)

                loaded = sem("loaded")
                small_loaded = sem("small_loaded")
                masks = sem("masks")
                masks_done = sem("masks_done")
                split_moved = sem("split_moved")
                split_ready = sem("split_ready")
                sums_ready = sem("sums_ready")
                total_ready = sem("total_ready")
                tern_ready = sem("tern_ready")
                transposed = sem("transposed")

                block = nc.Block()
                blk = block.__enter__()

                def row(ap):
                    n = ap.shape[0]
                    return bass.AP(tensor=ap.tensor, offset=ap.offset, ap=[[0, P], [1, n]])

                @blk.sync
                def _(sp):
                    for dst, src in ((x_res[:, :, :], x_dram), (wr_in[:, :], wr),
                                     (fw1_in[:, :, :], fw1.rearrange("(t p) d -> p t d", p=P)),
                                     (fw2_in[:, :], fw2), (aw_in[:, :, :], aw.rearrange("(t p) d -> p t d", p=P)),
                                     (b1_in[:, :], b1), (gam_in[:, :], row(gamma)), (bet_in[:, :], row(beta)),
                                     (fb2_in[:, :], row(fb2))):
                        sp.dma_start(dst, src).then_inc(loaded, 16)
                    sp.wait_ge(split_ready, 1)
                    for r in range(NPART):
                        sp.dma_start(b1_parts[r * E:(r + 1) * E, :], b1_split[:, r, :]).then_inc(split_moved, 16)
                    sp.wait_ge(split_moved, 16 * NPART)
                    sp.wait_ge(loaded, 16 * 9)

                @blk.scalar
                def _(act):
                    for dst, src in ((w_qkv0[:, 0, :], wq), (w_qkv0[:, 1, :], wk), (w_qkv0[:, 2, :], wv),
                                     (wo_sb[:, :], wo), (w1_sb[:, :, :], w1.rearrange("e d i -> d e i")),
                                     (wo2_sb[:, :, :], wo2.rearrange("(t p) d -> p t d", p=P)),
                                     (bo_bc[:, :], row(bo)), (bo2_bc[:, :], row(bo2)),
                                     (bv_bc[:, :], row(ab[2 * D:3 * D])),
                                     (col_in[0:2, :], ab[0:2 * D].rearrange("(t p) -> t p", p=P)),
                                     (col_in[2:2 + HT, :], fb1.rearrange("(t p) -> t p", p=P))):
                        act.dma_start(dst, src).then_inc(small_loaded, 16)
                    act.wait_ge(small_loaded, 16 * 11)

                @blk.gpsimd
                def _(pool):
                    pool.memset(ident[:, :], 0.0).then_inc(masks, 1)
                    pool.memset(ident_bf[:, :], 0.0).then_inc(masks, 1)
                    pool.memset(causal_add[:, :], 0.0).then_inc(masks, 1)
                    pool.memset(later_keys[:, :], 0.0).then_inc(masks, 1)
                    pool.memset(ones_mat[:, :], 1.0).then_inc(masks_done, 1)
                    pool.wait_ge(masks, 4)
                    pool.affine_select(out=ident[:, :], in_=ident[:, :], compare_op=ALU.not_equal, fill=1.0,
                                       base=0, pattern=[[-1, P]], channel_multiplier=1).then_inc(masks_done, 1)
                    pool.affine_select(out=ident_bf[:, :], in_=ident_bf[:, :], compare_op=ALU.not_equal, fill=1.0,
                                       base=0, pattern=[[-1, P]], channel_multiplier=1).then_inc(masks_done, 1)
                    pool.affine_select(out=causal_add[:, CH - P:CH], in_=causal_add[:, CH - P:CH],
                                       compare_op=ALU.is_ge, fill=NEG, base=0, pattern=[[-1, P]],
                                       channel_multiplier=1).then_inc(masks_done, 1)
                    pool.affine_select(out=later_keys[:, :], in_=later_keys[:, :], compare_op=ALU.is_ge, fill=NEG,
                                       base=0, pattern=[[1, P]], channel_multiplier=-1).then_inc(masks_done, 1)
                    pool.iota(rank[:, :], pattern=[[-1, E]], base=E, channel_multiplier=0,
                              allow_small_or_imprecise_dtypes=True).then_inc(masks_done, 1)
                    for n, lo in enumerate((32, 96)):
                        pool.wait_ge(masks_done, 6 + n)
                        pool.memset(k_slots[lo:lo + 32, :, :], 1.0).then_inc(masks_done, 1)

                @blk.vector
                def _(dve):
                    own = dve_chain.on(dve)
                    own(dve.memset(v_aug[:, :, :, :], 0.0))
                    own.wait()
                    own(dve.memset(v_aug[:, :, :, DH:DH + 1], 1.0))
                    dve.wait_ge(loaded, 16 * 9)
                    dve.tensor_reduce(abs_sum[:, 0:1], fw1_in[:, :, :], axis=AX.XY, op=ALU.add,
                                      apply_absolute_value=True).then_inc(sums_ready, 1)
                    dve.tensor_reduce(abs_sum[:, 1:2], fw2_in[:, :], axis=AX.X, op=ALU.add,
                                      apply_absolute_value=True).then_inc(sums_ready, 1)
                    own(dve.tensor_copy(b1_split[:, 0, :], b1_in[:, :]))
                    own.wait()
                    own(dve.tensor_tensor(b1_rest[:, :], b1_in[:, :], b1_split[:, 0, :], ALU.subtract))
                    own.wait()
                    own(dve.tensor_copy(b1_split[:, 1, :], b1_rest[:, :]))
                    own.wait()
                    dve.tensor_tensor(b1_split[:, 2, :], b1_rest[:, :], b1_split[:, 1, :],
                                      ALU.subtract).then_inc(split_ready, 1)
                    dve.tensor_scalar(gamma_half[:, :], gam_in[:, :], 0.5, None, ALU.mult)
                    dve.tensor_scalar(beta_half[:, :], bet_in[:, :], 0.5, None, ALU.mult)
                    dve.tensor_scalar(fb2_half[:, :], fb2_in[:, :], 0.5, None, ALU.mult)
                    dve.wait_ge(total_ready, 1)
                    for s, sign in ((0, 0.5), (1, -0.5)):
                        own(dve.tensor_scalar(half_gamma[:, s, :], psum[:, 0, 0:2], 1.0 / (HID * D), 1e-5,
                                              ALU.mult, ALU.add))
                        own.wait()
                        own(dve.tensor_scalar(half_gamma[:, s, :], half_gamma[:, s, :], sign, None, ALU.mult))
                    own.wait()
                    fw1_flat = fw1_in[:, :, :].rearrange("p t d -> p (t d)")
                    for m, src in ((0, fw1_flat), (1, fw2_in[:, :])):
                        own(dve.tensor_scalar(below[:, m, :], src, half_gamma[:, 1, m:m + 1], None, ALU.is_lt))
                        own.wait()
                        dve.scalar_tensor_tensor(out=tern[:, m, :], in0=src, scalar=half_gamma[:, 0, m:m + 1],
                                                 in1=below[:, m, :], op0=ALU.is_gt,
                                                 op1=ALU.subtract).then_inc(tern_ready, 1)
                    dve.wait_ge(transposed, 1)
                    dve.tensor_copy(tw1_t[:, :, :], psum[:, 1, :].rearrange("p (t f) -> p t f", t=HT))
                    dve.tensor_copy(tw2_t[:, :, :], psum[:, 2, :].rearrange("p (t d) -> p t d", t=HT))
                    dve.tensor_copy(w_qkv1[:, :, :], psum[:, 3, 0:3 * D].rearrange("p (t d) -> p t d", t=3))
                    dve.tensor_copy(wr_t[:, :], psum[:, 4, 0:E])
                    dve.tensor_copy(bias_cols[:, :], psum[:, 5, 0:2 + HT])

                @blk.tensor
                def _(pe):
                    pe.wait_ge(masks_done, 6)
                    pe.wait_ge(sums_ready, 2)
                    pe.matmul(psum[:, 0, 0:2], ones_mat[:, :], abs_sum[:, :], start=True,
                              stop=True).then_inc(total_ready, 1)
                    pe.wait_ge(loaded, 16 * 9)
                    for t in range(3):
                        pe.transpose(psum[:, 3, t * P:(t + 1) * P], aw_in[:, t, :], ident[:, :])
                    pe.transpose(psum[:, 4, 0:E], wr_in[:, :], ident[0:E, 0:E])
                    pe.wait_ge(small_loaded, 16 * 11)
                    pe.transpose(psum[:, 5, 0:2 + HT], col_in[:, :], ident[0:2 + HT, 0:2 + HT])
                    pe.wait_ge(tern_ready, 2)
                    for t in range(HT):
                        pe.transpose(psum[:, 1, t * P:(t + 1) * P], tern[:, 0, t * D:(t + 1) * D], ident[:, :])
                    for t in range(HT):
                        last = pe.transpose(psum[:, 2, t * P:(t + 1) * P], tern[:, 1, t * P:(t + 1) * P], ident[:, :])
                    last.then_inc(transposed, 1)

                block.__exit__(None, None, None)

        class NormScratch:
            def __init__(self, where):
                self.stats = sb("ln_stats", [P, NB, 6], where=where)
                self.mean_var = sb("ln_mean_var", [P, NB, 2], where=where)
                self.v = sb("ln_v", [P, NB], where=where)
                self.rstd = sb("ln_rstd", [P, NB], where=where)
                self.tmp = sb("ln_tmp", [P, NB], where=where)

        def norm_stats(dve, own, s, src, b0, n):
            for b in range(b0, b0 + n):
                own(dve.bn_stats(s.stats[:, b, :], src[:, b, :]))
            own.wait()
            for b in range(b0, b0 + n):
                own(dve.bn_aggr(s.mean_var[:, b, :], s.stats[:, b, :]))
            own.wait()

        def norm_rstd(dve, own, s, eps, b0, n):
            v, r, t = s.v[:, b0:b0 + n], s.rstd[:, b0:b0 + n], s.tmp[:, b0:b0 + n]
            own(dve.tensor_scalar(v, s.mean_var[:, b0:b0 + n, 1], eps, None, ALU.add))
            own.wait()
            own(dve.tensor_scalar(t.bitcast(I32), v.bitcast(I32), 1, None, ALU.arith_shift_right))
            own.wait()
            own(dve.tensor_scalar(r.bitcast(I32), t.bitcast(I32), -1.0, float(0x5F3759DF), ALU.mult, ALU.add))
            own.wait()
            for _ in range(3):
                own(dve.tensor_tensor(t, r, r, ALU.mult))
                own.wait()
                own(dve.tensor_tensor(t, t, v, ALU.mult))
                own.wait()
                own(dve.tensor_scalar(t, t, -0.5, 1.5, ALU.mult, ALU.add))
                own.wait()
                own(dve.tensor_tensor(r, r, t, ALU.mult))
                own.wait()

        def norm_apply(dve, s, dst, src, b):
            return dve.tensor_scalar(dst[:, b, :], src[:, b, :], s.mean_var[:, b, 0:1], s.rstd[:, b:b + 1],
                                     ALU.subtract, ALU.mult)

        def bcast_blocks(tile2d, n):
            return tile2d[:, :].rearrange("p (a d) -> p a d", a=1).broadcast_to([P, n, D])

        def expert_layer():
            local = ExitStack()
            with local:
                s1, s2 = NormScratch(local), NormScratch(local)
                xn = sb("xn", [P, NB, D], where=local)
                xn_t = sb("xn_t", [P, T], where=local)
                xn_bias = sb("xn_bias", [P, NB, D], where=local)
                x_beta = sb("x_beta", [P, NB, D], where=local)
                logit = sb("logit", [P, NB, E], where=local)
                top = sb("top", [P, NB], where=local)
                tied = sb("tied", [P, NB, E], where=local)
                onehot = sb("onehot", [P, NB, NPART * E], BF16, where=local)
                onehot_t = sb("onehot_t", [NPART * E, T], BF16, where=local)
                NX = 4
                x_mask = sb("x_mask", [P, NX, CH], where=local)
                h_t = sb("h_t", [P, 2, HT, CH], where=local)
                y = xn_bias

                xn_ready, xnt_psum, xnt_ready = sem("xn_ready"), sem("xnt_psum"), sem("xnt_ready")
                logits_done, onehot_ready = sem("logits_done"), sem("onehot_ready")
                oht_psum, oht_ready = sem("oht_psum"), sem("oht_ready")
                mask_psum, xmask_ready, experts_done = sem("mask_psum"), sem("xmask_ready"), sem("experts_done")
                gelu_done, down_done, y_ready = sem("gelu_done"), sem("down_done"), sem("y_ready")
                pool_pre, expert_mm = sem("pool_pre"), sem("expert_mm")
                block = nc.Block()
                blk = block.__enter__()

                @blk.tensor
                def _(pe):
                    for n in range(NCH):
                        pe.wait_ge(xn_ready, BPC * (n + 1))
                        for i in range(BPC):
                            last = pe.transpose(psum[:, n, i * P:(i + 1) * P], xn[:, n * BPC + i, :], ident[:, :])
                        last.then_inc(xnt_psum, 1)
                    for n in range(NCH):
                        pe.wait_ge(xnt_ready, n + 1)
                        for i in range(BPC):
                            b = n * BPC + i
                            last = pe.matmul(psum[:, 4, b * E:(b + 1) * E], xn_t[:, b * P:(b + 1) * P], wr_t[:, :],
                                             start=True, stop=True)
                    last.then_inc(logits_done, 1)
                    pe.wait_ge(onehot_ready, NPART)
                    for n in range(NCH):
                        if n >= 2:
                            pe.wait_ge(oht_ready, n - 1)
                        bank = psum[0:NPART * E, 5 + n % 2, 0:CH // 2].bitcast(BF16)
                        for i in range(BPC):
                            last = pe.transpose(bank[:, i * P:(i + 1) * P], onehot[:, n * BPC + i, :], ident_bf[:, :])
                        last.then_inc(oht_psum, 1)

                    def masks_of(k):
                        n, e = divmod(k, E)
                        if k >= 2:
                            pe.wait_ge(xmask_ready, k - 1)
                        elif k == 0:
                            pe.wait_ge(oht_ready, NCH)
                        for i in range(BPC):
                            b = n * BPC + i
                            last = pe.matmul(psum[:, 4 + k % 2, i * P:(i + 1) * P],
                                             onehot[:, b, e:e + 1].broadcast_to([P, P]), ident_bf[:, :],
                                             start=True, stop=True)
                        last.then_inc(mask_psum, 1)

                    def down(n):
                        pe.wait_ge(gelu_done, HT * (n + 1))
                        if n >= 2:
                            pe.wait_ge(y_ready, n - 1)
                        for i in range(BPC):
                            for t in range(HT):
                                last = pe.matmul(psum[:, 6 + n % 2, i * D:(i + 1) * D],
                                                 h_t[:, n % 2, t, i * P:(i + 1) * P], wo2_sb[:, t, :],
                                                 start=(t == 0), stop=(t == HT - 1))
                        last.then_inc(down_done, 1)

                    masks_of(0)
                    for n in range(NCH):
                        for e in range(E):
                            k = n * E + e
                            if k + 1 < NCH * E:
                                masks_of(k + 1)
                            pe.wait_ge(xmask_ready, k + 1)
                            if e == 0 and n >= 1:
                                pe.wait_ge(gelu_done, HT * n)
                            for t in range(HT):
                                last = pe.matmul(psum[:, t, :], w1_sb[:, e, t * P:(t + 1) * P], x_mask[:, k % NX, :],
                                                 start=(e == 0), stop=False)
                            last.then_inc(expert_mm, 1)
                            if e == 1 and n >= 1:
                                down(n - 1)
                        for t in range(HT):
                            pe.matmul(psum[:, t, :], b1_parts[:, t * P:(t + 1) * P], onehot_t[:, n * CH:(n + 1) * CH],
                                      start=False, stop=True).then_inc(experts_done, 1)
                    down(NCH - 1)

                @blk.scalar
                def _(act):
                    for n in range(NCH):
                        act.wait_ge(xnt_psum, n + 1)
                        act.copy(xn_t[:, n * CH:(n + 1) * CH], psum[:, n, :]).then_inc(xnt_ready, 1)
                    for n in range(NCH):
                        act.wait_ge(oht_psum, n + 1)
                        act.copy(onehot_t[:, n * CH:(n + 1) * CH],
                                 psum[0:NPART * E, 5 + n % 2, 0:CH // 2].bitcast(BF16)).then_inc(oht_ready, 1)
                    for n in range(NCH):
                        for t in range(HT):
                            act.wait_ge(experts_done, n * HT + t + 1)
                            if n >= 2:
                                act.wait_ge(down_done, n - 1)
                            act.activation(h_t[:, n % 2, t, :], psum[:, t, :], ACT.Gelu).then_inc(gelu_done, 1)

                @blk.gpsimd
                def _(pool):
                    for n in range(NCH):
                        lo, hi = n * BPC, (n + 1) * BPC
                        pool.wait_ge(xn_ready, BPC * (n + 1))
                        pool.tensor_tensor(xn_bias[:, lo:hi, :], xn[:, lo:hi, :], bcast_blocks(bo2_bc, BPC),
                                           ALU.add).then_inc(pool_pre, 1)
                        pool.tensor_tensor(x_beta[:, lo:hi, :], x_res[:, lo:hi, :], bcast_blocks(beta_half, BPC),
                                           ALU.add).then_inc(pool_pre, 1)

                @blk.vector
                def _(dve):
                    own = dve_chain.on(dve)
                    norm_stats(dve, own, s1, x_res, 0, NB)
                    norm_rstd(dve, own, s1, 1e-5, 0, NB)
                    for b in range(NB):
                        norm_apply(dve, s1, xn, x_res, b).then_inc(xn_ready, 1)
                    dve.wait_ge(logits_done, 1)
                    own(dve.tensor_copy(logit[:, :, :], psum[:, 4, 0:NB * E].rearrange("p (b e) -> p b e", e=E)))
                    own.wait()

                    def per_block(ap):
                        return ap.rearrange("p (b a) -> p b a", a=1).broadcast_to([P, NB, E])

                    own(dve.tensor_reduce(top[:, :], logit[:, :, :], axis=AX.X, op=ALU.max))
                    own.wait()
                    own(dve.tensor_tensor(tied[:, :, :], logit[:, :, :], per_block(top[:, :]), ALU.is_ge))
                    own.wait()
                    rank_b = rank[:, :].rearrange("p (a e) -> p a e", a=1).broadcast_to([P, NB, E])
                    own(dve.tensor_tensor(tied[:, :, :], tied[:, :, :], rank_b, ALU.mult))
                    own.wait()
                    own(dve.tensor_reduce(top[:, :], tied[:, :, :], axis=AX.X, op=ALU.max))
                    own.wait()
                    for r in range(NPART):
                        dve.tensor_tensor(onehot[:, :, r * E:(r + 1) * E], tied[:, :, :], per_block(top[:, :]),
                                          ALU.is_equal).then_inc(onehot_ready, 1)

                    def finish(n):
                        lo, hi = n * BPC, (n + 1) * BPC
                        dve.wait_ge(down_done, n + 1)
                        dve.wait_ge(pool_pre, 2 * NCH)
                        dve.tensor_tensor(y[:, lo:hi, :], psum[:, 6 + n % 2, :].rearrange("p (b d) -> p b d", d=D),
                                          xn_bias[:, lo:hi, :], ALU.add).then_inc(y_ready, 1)
                        dve.wait_ge(y_ready, n + 1)
                        norm_stats(dve, own, s2, y, lo, BPC)
                        norm_rstd(dve, own, s2, 1e-12, lo, BPC)
                        for b in range(lo, hi):
                            own(norm_apply(dve, s2, xn, y, b))
                        own.wait()
                        own(dve.tensor_tensor(y[:, lo:hi, :], xn[:, lo:hi, :], bcast_blocks(gamma_half, BPC), ALU.mult))
                        own.wait()
                        own(dve.tensor_tensor(x_res[:, lo:hi, :], y[:, lo:hi, :], x_beta[:, lo:hi, :], ALU.add))

                    for k in range(NCH * E):
                        n = k // E
                        dve.wait_ge(mask_psum, k + 1)
                        if k >= NX:
                            dve.wait_ge(expert_mm, k - NX + 1)
                        dve.tensor_tensor(x_mask[:, k % NX, :], psum[:, 4 + k % 2, :], xn_t[:, n * CH:(n + 1) * CH],
                                          ALU.mult).then_inc(xmask_ready, 1)
                        if k % E == 4 and n >= 1:
                            finish(n - 1)
                    finish(NCH - 1)

                block.__exit__(None, None, None)

        def ternary_layer(last_layer):
            local = ExitStack()
            with local:
                s1 = NormScratch(local)
                xn = sb("xn", [P, NB, D], where=local)
                xn_t = sb("xn_t", [P, T], where=local)
                x_bias = sb("x_bias", [P, NB, D], where=local)
                h_t = sb("h_t", [P, 2, HT, CH], where=local)
                xn_ready, xnt_psum, xnt_ready = sem("xn_ready"), sem("xnt_psum"), sem("xnt_ready")
                up_done, relu_done, down_done = sem("up_done"), sem("relu_done"), sem("down_done")
                pool_pre, x_ready, stored = sem("pool_pre"), sem("x_ready"), sem("stored")
                block = nc.Block()
                blk = block.__enter__()

                @blk.tensor
                def _(pe):
                    def features(n):
                        pe.wait_ge(xn_ready, BPC * (n + 1))
                        if n >= 1:
                            pe.wait_ge(xnt_ready, n)
                        for i in range(BPC):
                            last = pe.transpose(psum[:, 4, i * P:(i + 1) * P], xn[:, n * BPC + i, :], ident[:, :])
                        last.then_inc(xnt_psum, 1)

                    def down(n):
                        if n >= 2:
                            pe.wait_ge(x_ready, n - 1)
                        pe.wait_ge(relu_done, HT * (n + 1))
                        for i in range(BPC):
                            for t in range(HT):
                                last = pe.matmul(psum[:, 6 + n % 2, i * D:(i + 1) * D],
                                                 h_t[:, n % 2, t, i * P:(i + 1) * P], tw2_t[:, t, :],
                                                 start=(t == 0), stop=(t == HT - 1))
                        last.then_inc(down_done, 1)

                    features(0)
                    for n in range(NCH):
                        pe.wait_ge(xnt_ready, n + 1)
                        for t in range(HT):
                            if n >= 1:
                                pe.wait_ge(relu_done, HT * (n - 1) + t + 1)
                            pe.matmul(psum[:, t, :], tw1_t[:, t, :], xn_t[:, n * CH:(n + 1) * CH],
                                      start=True, stop=True).then_inc(up_done, 1)
                        if n + 1 < NCH:
                            features(n + 1)
                        if n >= 1:
                            down(n - 1)
                    down(NCH - 1)

                @blk.scalar
                def _(act):
                    for n in range(NCH):
                        act.wait_ge(xnt_psum, n + 1)
                        act.copy(xn_t[:, n * CH:(n + 1) * CH], psum[:, 4, :]).then_inc(xnt_ready, 1)
                        for t in range(HT):
                            act.wait_ge(up_done, n * HT + t + 1)
                            if n >= 2:
                                act.wait_ge(down_done, n - 1)
                            act.activation(h_t[:, n % 2, t, :], psum[:, t, :], ACT.Relu,
                                           bias=fb1_col[:, t:t + 1]).then_inc(relu_done, 1)

                @blk.gpsimd
                def _(pool):
                    for n in range(NCH):
                        lo, hi = n * BPC, (n + 1) * BPC
                        pool.tensor_tensor(x_bias[:, lo:hi, :], x_res[:, lo:hi, :], bcast_blocks(fb2_half, BPC),
                                           ALU.add).then_inc(pool_pre, 1)

                @blk.vector
                def _(dve):
                    own = dve_chain.on(dve)
                    norm_stats(dve, own, s1, x_res, 0, NB)
                    norm_rstd(dve, own, s1, 1e-5, 0, NB)
                    for b in range(NB):
                        norm_apply(dve, s1, xn, x_res, b).then_inc(xn_ready, 1)
                    dve.wait_ge(xn_ready, NB)
                    dve.wait_ge(pool_pre, NCH)
                    for n in range(NCH):
                        lo, hi = n * BPC, (n + 1) * BPC
                        dve.wait_ge(down_done, n + 1)
                        dve.scalar_tensor_tensor(out=x_res[:, lo:hi, :].rearrange("p b d -> p (b d)"),
                                                 in0=psum[:, 6 + n % 2, :], scalar=0.5,
                                                 in1=x_bias[:, lo:hi, :].rearrange("p b d -> p (b d)"),
                                                 op0=ALU.mult, op1=ALU.add).then_inc(x_ready, 1)

                @blk.sync
                def _(sp):
                    if last_layer:
                        for n in range(NCH):
                            lo, hi = n * BPC, (n + 1) * BPC
                            sp.wait_ge(x_ready, n + 1)
                            sp.dma_start(out_dram[:, lo:hi, :], x_res[:, lo:hi, :]).then_inc(stored, 16)
                        sp.wait_ge(stored, 16 * NCH)

                block.__exit__(None, None, None)

        LOTS = [[(0, c)] for c in range(NCH)]
        for g in range(1, NG):
            LOTS += [[(g, 0), (g, 3)], [(g, 1), (g, 2)]]
        STEPS = [s for lot in LOTS for s in lot]

        def quads_of(step):
            return [(step, j) for j in range(BPC * (step[1] + 1))]

        def max_units_of(step):
            return [(step, i, kc, h) for i in range(BPC) for kc in range(step[1] + 1) for h in range(G)]

        TURNS = [(None, max_units_of(LOTS[0][0])), (None, [])]
        for n, lot in enumerate(LOTS):
            quads = [q for s in lot for q in quads_of(s)]
            units = [u for s in (LOTS[n + 1] if n + 1 < len(LOTS) else []) for u in max_units_of(s)]
            over = len(quads) - 2 if n + 1 < len(LOTS) and len(LOTS[n + 1]) == 1 else len(quads)
            for i, q in enumerate(quads):
                TURNS.append((q, units[len(units) * i // over:len(units) * (i + 1) // over]))
        TURNS += [(None, [])] * 3

        def attention_layer(w_qkv, biased, projected):
            local = ExitStack()
            with local:
                s1 = NormScratch(local)
                xn = sb("xn", [P, NB, D], where=local)
                ctx = xn
                xn_t = sb("xn_t", [P, T], where=local)
                NP = 6
                probs = sb("probs", [P, NP, 2, CH], where=local)
                parts = probs[:, 0:NP // 2, :, :].rearrange("p a b c -> p (a b c)").bitcast(BF16)
                qf = sb("qf", [P, 2, CH], where=local)
                rest = sb("rest", [P, 2, CH], where=local)
                qk_parts = sb("qk_parts", [P, 2, NPART, CH], BF16, where=local)
                out_t = sb("out_t", [P, 2, CH], where=local)
                recip = sb("recip", [P, 2, BPC, G], where=local)
                junk = sb("junk", [P, 2, CH], where=local)
                part_max = sb("part_max", [P, 2, G, BPC, NCH], where=local)
                neg_max = sb("neg_max", [P, 2, G * BPC], where=local)
                nm_rest = sb("nm_rest", [G * BPC, P], where=local)
                nm_parts = sb("nm_parts", [G * BPC, 2, NPART, P], BF16, where=local)

                xn_ready, xnt_psum, xnt_ready = sem("xn_ready"), sem("xnt_psum"), sem("xnt_ready")
                proj_done, qf_ready, hi_ready, rest_ready = sem("proj_done"), sem("qf_ready"), sem("hi_ready"), sem("rest_ready")
                mid_ready, lo_ready, v_psum, v_ready = sem("mid_ready"), sem("lo_ready"), sem("v_psum"), sem("v_ready")
                parts_stored = [sem(f"parts_stored{i}") for i in range(2)]
                slots_landed = sem("slots_landed")
                block = nc.Block()
                blk = block.__enter__()

                PROJ = [(n, m) for n in range(NCH) for m in range(2)]

                @blk.tensor
                def _(pe):
                    for n in range(NCH):
                        pe.wait_ge(xn_ready, BPC * (n + 1))
                        for i in range(BPC):
                            last = pe.transpose(psum[:, n, i * P:(i + 1) * P], xn[:, n * BPC + i, :], ident[:, :])
                        last.then_inc(xnt_psum, 1)
                    for k, (n, m) in enumerate(PROJ):
                        pe.wait_ge(xnt_ready, n + 1)
                        if k >= 2:
                            pe.wait_ge(hi_ready, k - 1)
                            pe.wait_ge(qf_ready, k - 1)
                        pe.matmul(psum[:, 4 + k % 2, :], w_qkv[:, m, :], xn_t[:, n * CH:(n + 1) * CH],
                                  start=True, stop=True).then_inc(proj_done, 1)
                    for n in range(NCH):
                        if n >= 2:
                            pe.wait_ge(v_ready, n - 1)
                        for i in range(BPC):
                            b = n * BPC + i
                            last = pe.matmul(psum[:, 6 + n % 2, i * D:(i + 1) * D], xn_t[:, b * P:(b + 1) * P],
                                             w_qkv[:, 2, :], start=True, stop=True)
                        last.then_inc(v_psum, 1)

                @blk.scalar
                def _(act):
                    for n in range(NCH):
                        act.wait_ge(xnt_psum, n + 1)
                        act.copy(xn_t[:, n * CH:(n + 1) * CH], psum[:, n, :]).then_inc(xnt_ready, 1)
                    for k, (n, m) in enumerate(PROJ):
                        act.wait_ge(proj_done, k + 1)
                        if k >= 2:
                            act.wait_ge(rest_ready, k - 1)
                            act.wait_ge(parts_stored[k % 2], 16 * NPART * (k // 2))
                        if biased:
                            act.activation(qf[:, k % 2, :], psum[:, 4 + k % 2, :], ACT.Identity,
                                           bias=qk_bias[:, m:m + 1]).then_inc(qf_ready, 1)
                        else:
                            act.copy(qf[:, k % 2, :], psum[:, 4 + k % 2, :]).then_inc(qf_ready, 1)
                        act.wait_ge(qf_ready, k + 1)
                        act.copy(qk_parts[:, k % 2, 0, :], qf[:, k % 2, :]).then_inc(hi_ready, 1)
                        act.wait_ge(rest_ready, k + 1)
                        act.copy(qk_parts[:, k % 2, 1, :], rest[:, k % 2, :]).then_inc(mid_ready, 1)

                @blk.vector
                def _(dve):
                    own = dve_chain.on(dve)
                    norm_stats(dve, own, s1, x_res, 0, NB)
                    norm_rstd(dve, own, s1, 1e-5, 0, NB)
                    for b in range(NB):
                        norm_apply(dve, s1, xn, x_res, b).then_inc(xn_ready, 1)
                    for k, (n, m) in enumerate(PROJ):
                        dve.wait_ge(hi_ready, k + 1)
                        if k >= 2:
                            dve.wait_ge(lo_ready, k - 1)
                        dve.tensor_tensor(rest[:, k % 2, :], qf[:, k % 2, :], qk_parts[:, k % 2, 0, :],
                                          ALU.subtract).then_inc(rest_ready, 1)
                        if k >= 1:
                            dve.wait_ge(mid_ready, k)
                            dve.tensor_tensor(qk_parts[:, (k - 1) % 2, 2, :], rest[:, (k - 1) % 2, :],
                                              qk_parts[:, (k - 1) % 2, 1, :], ALU.subtract).then_inc(lo_ready, 1)
                    k = len(PROJ)
                    dve.wait_ge(mid_ready, k)
                    dve.tensor_tensor(qk_parts[:, (k - 1) % 2, 2, :], rest[:, (k - 1) % 2, :],
                                      qk_parts[:, (k - 1) % 2, 1, :], ALU.subtract).then_inc(lo_ready, 1)
                    for n in range(NCH):
                        dve.wait_ge(v_psum, n + 1)
                        dst = v_aug[:, n * BPC:(n + 1) * BPC, :, 0:DH]
                        src = psum[:, 6 + n % 2, :].rearrange("p (b h d) -> p b h d", h=H, d=DH)
                        if biased:
                            for i in range(BPC):
                                last = dve.tensor_tensor(dst[:, i], src[:, i],
                                                         bv_bc[:, :].rearrange("p (h d) -> p h d", d=DH), ALU.add)
                        else:
                            last = dve.tensor_copy(dst, src)
                        last.then_inc(v_ready, 1)

                @blk.sync
                def _(sp):
                    for k, (n, m) in enumerate(PROJ):
                        sp.wait_ge(lo_ready, k + 1)
                        for r in range(NPART):
                            sp.dma_start(part_dram[m][r][:, n * CH:(n + 1) * CH],
                                         qk_parts[:, k % 2, r, :]).then_inc(parts_stored[k % 2], 16)
                    for i in range(2):
                        sp.wait_ge(parts_stored[i], 16 * NPART * len(PROJ) // 2)
                    for g in range(NG):
                        for par in range(2):
                            row = SLOT * par
                            for kp, reps in enumerate(TERMS):
                                for qp in range(reps):
                                    for slots, src in ((q_slots, part_dram[0][qp]), (k_slots, part_dram[1][kp])):
                                        rows = src.rearrange("(a two d) t -> two d a t", two=2, d=DH)
                                        sp.dma_start(slots[row:row + DH, 2 * g:2 * g + 2, :],
                                                     rows[par, :, 2 * g:2 * g + 2, :]).then_inc(slots_landed, 16)
                                    row += DH
                    sp.wait_ge(slots_landed, 16 * NG * 4 * sum(TERMS))

                block.__exit__(None, None, None)

                reduce_done, scores_max = sem("reduce_done"), sem("scores_max")
                negmax_ready, negmax_t, negmax_split = sem("negmax_ready"), sem("negmax_t"), sem("negmax_split")
                negmax_stored = [sem(f"negmax_stored{i}") for i in range(2)]
                negmax_landed = [sem(f"negmax_landed{i}") for i in range(4)]
                scores_done, exp_done, pv_done = sem("scores_done"), sem("exp_done"), sem("pv_done")
                pv_step_done, out_copied, out_t_psum, ctx_ready = sem("pv_step_done"), sem("out_copied"), sem("out_t_psum"), sem("ctx_ready")
                misc_read = sem("misc_read")
                S_BANKS, M_BANKS, O_BANK, MISC = 0, 4, 6, 7

                block = nc.Block()
                blk = block.__enter__()

                def head_rows(h, n):
                    return slice(SLOT * (h % 2), SLOT * (h % 2) + n)

                step_no = {s: i for i, s in enumerate(STEPS)}
                quad_no = {q: i for i, q in enumerate(q for q, _ in TURNS if q)}
                diagonal = {q for q in quad_no if q[1] >= BPC * q[0][1]}
                unit_no = {u: i for i, u in enumerate(u for _, us in TURNS for u in us)}
                last_unit = {u[0]: i for u, i in unit_no.items()}

                def first_query(q):
                    (_, c), j = q
                    return max(0, j - BPC * c) * P

                def late_work():
                    plan, ended_m, ended_q = [], [], []
                    for q, units in TURNS:
                        m_now = [s for s in STEPS if any(unit_no[u] == last_unit[s] for u in units if u[0] == s)]
                        q_now = [q[0]] if q and q[1] == BPC * (q[0][1] + 1) - 1 else []
                        plan.append((m_now, ended_m[-1] if ended_m else [], ended_q[-1] if ended_q else [],
                                     ended_q[-2] if len(ended_q) > 1 else []))
                        ended_m.append(m_now)
                        ended_q.append(q_now)
                    return plan

                PLAN = late_work()

                @blk.tensor
                def _(pe):
                    misc = 0

                    def free_misc():
                        if misc:
                            pe.wait_ge(misc_read, misc)

                    previous = None
                    for (q, units), (_, turn_max, _, turn_out) in zip(TURNS, PLAN):
                        if q:
                            (g, c), j = q
                            n = quad_no[q]
                            off = first_query(q)
                            if j == 0:
                                pe.wait_ge(negmax_landed[step_no[q[0]] % 4], 32 * (step_no[q[0]] // 4 + 1))
                            for pr in range(2):
                                tile = 2 * n + pr
                                if tile >= 2:
                                    pe.wait_ge(exp_done, tile - 1)
                                for par in range(2):
                                    h = 2 * pr + par
                                    rows = head_rows(h, KROWS)
                                    last = pe.matmul(psum[:, S_BANKS + 2 * (tile % 2) + par, off:CH],
                                                     k_slots[rows, 2 * g + pr, j * P:(j + 1) * P],
                                                     q_slots[rows, 2 * g + pr, c * CH + off:(c + 1) * CH],
                                                     start=True, stop=q not in diagonal)
                                if q in diagonal:
                                    for par in range(2):
                                        last = pe.matmul(psum[:, S_BANKS + 2 * (tile % 2) + par, off:off + P],
                                                         ident_bf[:, :], later_keys[:, :], start=False, stop=True)
                                last.then_inc(scores_done, 1)
                        if previous:
                            (g, c), j = previous
                            n = quad_no[previous]
                            off = first_query(previous)
                            pe.wait_ge(exp_done, 2 * n + 2)
                            if j == 0 and step_no[previous[0]] >= 1:
                                pe.wait_ge(out_copied, step_no[previous[0]])
                            for h in range(G):
                                last = pe.matmul(psum[VW * h:VW * (h + 1), O_BANK, off:CH],
                                                 v_aug[:, j, G * g + h, :],
                                                 probs[:, (2 * n + h // 2) % NP, h % 2, off:CH],
                                                 start=(j == 0), stop=(j == BPC * (c + 1) - 1))
                            last.then_inc(pv_done, 1)
                        for u in units:
                            (g, c), i, kc, h = u
                            n = unit_no[u]
                            w = CH if kc < c else (i + 1) * P
                            rows = head_rows(h, QK_ROWS)
                            pair = 2 * g + h // 2
                            qb = BPC * c + i
                            if n >= 2:
                                pe.wait_ge(reduce_done, n - 1)
                            pe.matmul(psum[:, M_BANKS + n % 2, 0:w], q_slots[rows, pair, qb * P:(qb + 1) * P],
                                      k_slots[rows, pair, kc * CH:kc * CH + w],
                                      start=True, stop=True).then_inc(scores_max, 1)
                        for s in turn_max:
                            free_misc()
                            k = step_no[s]
                            pe.wait_ge(negmax_ready, k + 1)
                            pe.transpose(psum[0:G * BPC, MISC, 0:P], neg_max[:, k % 2, :],
                                         ident[:, :]).then_inc(negmax_t, 1)
                            misc += 1
                        for s in turn_out:
                            free_misc()
                            k = step_no[s]
                            pe.wait_ge(out_copied, k + 1)
                            for i in range(BPC):
                                last = pe.transpose(psum[:, MISC, i * P:(i + 1) * P], out_t[:, k % 2, i * P:(i + 1) * P],
                                                    ident[:, :])
                            last.then_inc(out_t_psum, 1)
                            misc += 1
                        previous = q

                @blk.scalar
                def _(act):
                    for (q, _), (_, _, copy_out, _) in zip(TURNS, PLAN):
                        if q:
                            n = quad_no[q]
                            off = first_query(q)
                            for pr in range(2):
                                tile = 2 * n + pr
                                act.wait_ge(scores_done, tile + 1)
                                if tile >= NP:
                                    act.wait_ge(pv_done, (tile - NP) // 2 + 1)
                                bank = S_BANKS + 2 * (tile % 2)
                                act.activation(probs[:, tile % NP, :, off:CH], psum[:, bank:bank + 2, off:CH],
                                               ACT.Exp, scale=SCALE).then_inc(exp_done, 1)
                        for s in copy_out:
                            k = step_no[s]
                            last_quad = quad_no[(s, BPC * (s[1] + 1) - 1)]
                            act.wait_ge(pv_done, last_quad + 1)
                            if k >= 2:
                                act.wait_ge(out_t_psum, k - 1)
                            act.copy(out_t[:, k % 2, :], psum[:, O_BANK, :]).then_inc(out_copied, 1)

                @blk.vector
                def _(dve):
                    own = dve_chain.on(dve)
                    misc = 0
                    for (_, units), (m_now, turn_max, _, turn_out) in zip(TURNS, PLAN):
                        for u in units:
                            s, i, kc, h = u
                            n = unit_no[u]
                            k = step_no[s]
                            dve.wait_ge(scores_max, n + 1)
                            dst = part_max[:, k % 2, h, i, kc:kc + 1]
                            if kc < s[1]:
                                dve.tensor_reduce(dst, psum[:, M_BANKS + n % 2, :], axis=AX.X,
                                                  op=ALU.max).then_inc(reduce_done, 1)
                            else:
                                w = (i + 1) * P
                                if n >= 1:
                                    dve.wait_ge(reduce_done, n)
                                dve.tensor_tensor_reduce(out=junk[:, n % 2, 0:w], in0=psum[:, M_BANKS + n % 2, 0:w],
                                                         in1=causal_add[:, CH - w:CH], scale=1.0, scalar=-3.0e38,
                                                         op0=ALU.add, op1=ALU.max,
                                                         accum_out=dst).then_inc(reduce_done, 1)
                        for s in m_now:
                            k = step_no[s]
                            dve.wait_ge(reduce_done, last_unit[s] + 1)
                            if k >= 2:
                                dve.wait_ge(negmax_t, k - 1)
                            dve.tensor_reduce(neg_max[:, k % 2, :],
                                              part_max[:, k % 2, :, :, 0:s[1] + 1].rearrange("p h i c -> p (h i) c"),
                                              axis=AX.X, op=ALU.max, negate=True).then_inc(negmax_ready, 1)
                        for s in turn_max:
                            k = step_no[s]
                            dve.wait_ge(negmax_t, k + 1)
                            if k >= 2:
                                dve.wait_ge(negmax_stored[k % 2], 16 * (k // 2))
                            src = psum[0:G * BPC, MISC, 0:P]
                            own(dve.tensor_copy(nm_parts[:, k % 2, 0, :], src))
                            own.wait()
                            dve.tensor_tensor(nm_rest[:, :], src, nm_parts[:, k % 2, 0, :],
                                              ALU.subtract).then_inc(misc_read, 1)
                            misc += 1
                            dve.wait_ge(misc_read, misc)
                            own(dve.tensor_copy(nm_parts[:, k % 2, 1, :], nm_rest[:, :]))
                            own.wait()
                            dve.tensor_tensor(nm_parts[:, k % 2, 2, :], nm_rest[:, :], nm_parts[:, k % 2, 1, :],
                                              ALU.subtract).then_inc(negmax_split, 1)
                            dve.wait_ge(negmax_split, k + 1)
                        for s in turn_out:
                            (g, c), k = s, step_no[s]
                            dve.wait_ge(out_t_psum, k + 1)
                            rows = psum[:, MISC, :].rearrange("p (b h w) -> p b h w", h=G, w=VW)
                            own(dve.reciprocal(recip[:, k % 2, :, :], rows[:, :, :, DH]))
                            own.wait()
                            r = recip[:, k % 2, :, :].rearrange("p b (h a) -> p b h a", a=1)
                            dst = ctx[:, c * BPC:(c + 1) * BPC, g * G * DH:(g + 1) * G * DH]
                            dve.tensor_tensor(dst.rearrange("p b (h d) -> p b h d", d=DH), rows[:, :, :, 0:DH],
                                              r.broadcast_to([P, BPC, G, DH]), ALU.mult).then_inc(misc_read, 1)
                            misc += 1
                            dve.wait_ge(misc_read, misc)

                @blk.sync
                def _(sp):
                    for k, (g, c) in enumerate(STEPS):
                        sp.wait_ge(negmax_split, k + 1)
                        sp.dma_start(negmax_dram[k].rearrange("r hi q -> hi r q"),
                                     nm_parts[:, k % 2, :, :]).then_inc(negmax_stored[k % 2], 16)
                        sp.wait_ge(negmax_stored[k % 2], 16 * (k // 2 + 1))
                        for par in range(2):
                            lo = SLOT * par + QK_ROWS
                            src = negmax_dram[k].rearrange("r (pr two i) q -> two r pr (i q)", pr=2, two=2)[par]
                            sp.dma_start(q_slots[lo:lo + NPART, 2 * g:2 * g + 2, c * CH:(c + 1) * CH],
                                         src).then_inc(negmax_landed[k % 4], 16)
                    for i in range(4):
                        sp.wait_ge(negmax_landed[i], 32 * len(STEPS[i::4]))

                block.__exit__(None, None, None)

                ct_psum, ct_ready, o_done = sem("ct_psum"), sem("ct_ready"), sem("o_done")
                block = nc.Block()
                blk = block.__enter__()

                if projected:
                    @blk.tensor
                    def _(pe):
                        for n in range(NCH):
                            for i in range(BPC):
                                last = pe.transpose(psum[:, n, i * P:(i + 1) * P], ctx[:, n * BPC + i, :], ident[:, :])
                            last.then_inc(ct_psum, 1)
                        for n in range(NCH):
                            pe.wait_ge(ct_ready, n + 1)
                            for i in range(BPC):
                                b = n * BPC + i
                                last = pe.matmul(psum[:, 4 + n, i * D:(i + 1) * D], xn_t[:, b * P:(b + 1) * P],
                                                 wo_sb[:, :], start=True, stop=True)
                            last.then_inc(o_done, 1)

                    @blk.scalar
                    def _(act):
                        for n in range(NCH):
                            act.wait_ge(ct_psum, n + 1)
                            act.copy(xn_t[:, n * CH:(n + 1) * CH], psum[:, n, :]).then_inc(ct_ready, 1)

                @blk.vector
                def _(dve):
                    own = dve_chain.on(dve)
                    for n in range(NCH):
                        lo, hi = n * BPC, (n + 1) * BPC
                        if projected:
                            own(dve.tensor_tensor(x_res[:, lo:hi, :], x_res[:, lo:hi, :], bcast_blocks(bo_bc, BPC), ALU.add))
                            own.wait()
                            dve.wait_ge(o_done, n + 1)
                            own(dve.tensor_tensor(x_res[:, lo:hi, :], psum[:, 4 + n, :].rearrange("p (b d) -> p b d", d=D),
                                                  x_res[:, lo:hi, :], ALU.add))
                        else:
                            own(dve.tensor_tensor(x_res[:, lo:hi, :], ctx[:, lo:hi, :], x_res[:, lo:hi, :], ALU.add))

                block.__exit__(None, None, None)

        setup()
        expert_layer()
        attention_layer(w_qkv0, biased=False, projected=True)
        expert_layer()
        ternary_layer(last_layer=False)
        attention_layer(w_qkv1, biased=True, projected=False)
        ternary_layer(last_layer=True)


_INS = ['L0_attn_x', 'L0_attn_wq', 'L0_attn_wk', 'L0_attn_wv', 'L0_attn_wo', 'L0_attn_bo', 'L0_ffn_Wr', 'L0_ffn_W1',
        'L0_ffn_b1', 'L0_ffn_Wo', 'L0_ffn_bo', 'L0_ffn_gamma', 'L0_ffn_beta', 'L1_attn_W', 'L1_attn_b', 'L1_ffn_W1',
        'L1_ffn_b1', 'L1_ffn_W2', 'L1_ffn_b2']
_OUT_SHAPE = (1, T, D)


def kernel(**inputs):
    import numpy as _np
    import concourse.bacc as _bacc
    from concourse import mybir as _mybir
    from concourse.bass_utils import run_bass_kernel_spmd as _run

    nc = _bacc.Bacc("TRN2", target_bir_lowering=False, num_devices=1)
    arrays, args = {}, []
    for name in _INS:
        a = _np.ascontiguousarray(inputs[name])
        arrays[f"in_{name}_dram"] = a
        args.append(nc.dram_tensor(f"in_{name}_dram", a.shape, _mybir.dt.from_np(a.dtype), kind="ExternalInput").ap())
    out = nc.dram_tensor("out_0_dram", _OUT_SHAPE, _mybir.dt.float32, kind="ExternalOutput").ap()
    macaron_layers(nc, *args, out)
    r = _run(nc, [arrays], core_ids=[0])
    return r.results[0]["out_0_dram"]
```

```python
from contextlib import ExitStack

import concourse.bass as bass
from concourse import mybir

F32 = mybir.dt.float32
BF16 = mybir.dt.bfloat16
I32 = mybir.dt.int32
ALU = mybir.AluOpType
ACT = mybir.ActivationFunctionType
AX = mybir.AxisListType

P = 128
T = 2048
D = 128
NB = T // P
CH = 512
NCH = T // CH
BPC = CH // P
H = 16
DH = D // H
G = 4
NG = H // G
PAIRS = H // 2
SCALE = float(DH) ** -0.5
E = 8
HID = 512
HT = HID // P
NEG = -1.0e30
NPART = 3
TERMS = (3, 2, 1)
QK_ROWS = DH * sum(TERMS)
KROWS = QK_ROWS + NPART
SLOT = 64
VW = 32


class Chain:

    def __init__(self, semaphore):
        self.semaphore, self.count = semaphore, 0

    def on(self, engine):
        self.engine = engine
        return self

    def __call__(self, instruction):
        instruction.then_inc(self.semaphore, 1)
        self.count += 1
        return instruction

    def wait(self):
        if self.count:
            self.engine.wait_ge(self.semaphore, self.count)


def macaron_layers(nc, x_in, wq, wk, wv, wo, bo, wr, w1, b1, wo2, bo2, gamma, beta,
                   aw, ab, fw1, fb1, fw2, fb2, out):
    stack = ExitStack()
    names = [0]

    def sb(name, shape, dt=F32, where=None):
        names[0] += 1
        return (where or stack).enter_context(nc.sbuf_tensor(f"{name}_{names[0]}", shape, dt))

    def sem(name):
        names[0] += 1
        return stack.enter_context(nc.semaphore(f"{name}_{names[0]}"))

    with stack:
        psum = stack.enter_context(nc.psum_tensor("psum", [P, 8, CH], F32))

        x_res = sb("x_res", [P, NB, D])
        ident = sb("ident", [P, P])
        ident_bf = sb("ident_bf", [P, P], BF16)
        causal_add = sb("causal_add", [P, CH])
        later_keys = sb("later_keys", [P, P], BF16)
        ones_mat = sb("ones_mat", [P, P])
        q_slots = sb("q_slots", [P, PAIRS, T], BF16)
        k_slots = sb("k_slots", [P, H, T], BF16)
        v_aug = sb("v_aug", [P, NB, H, DH + 1])
        w_qkv0 = sb("w_qkv0", [P, 3, D])
        w_qkv1 = sb("w_qkv1", [P, 3, D])
        wo_sb = sb("wo_sb", [P, D])
        bo_bc = sb("bo_bc", [P, D])
        bv_bc = sb("bv_bc", [P, D])
        bias_cols = sb("bias_cols", [P, 2 + HT])
        qk_bias, fb1_col = bias_cols[:, 0:2], bias_cols[:, 2:2 + HT]
        wr_t = sb("wr_t", [P, E])
        w1_sb = sb("w1_sb", [P, E, HID])
        b1_parts = sb("b1_parts", [NPART * E, HID], BF16)
        wo2_sb = sb("wo2_sb", [P, HT, D])
        bo2_bc = sb("bo2_bc", [P, D])
        gamma_half = sb("gamma_half", [P, D])
        beta_half = sb("beta_half", [P, D])
        rank = sb("rank", [P, E])
        tw1_t = sb("tw1_t", [P, HT, P])
        tw2_t = sb("tw2_t", [P, HT, D])
        fb2_half = sb("fb2_half", [P, D])

        dve_chain = Chain(sem("dve_own"))
        slot_dram = [nc.dram_tensor(f"{n}_rows", [H, sum(TERMS), DH, T], BF16, kind="Internal").ap() for n in ("q", "k")]
        ROW_PARTS = [[qp for reps in TERMS for qp in range(reps)], [kp for kp, reps in enumerate(TERMS) for _ in range(reps)]]
        negmax_dram = nc.dram_tensor("negmax", [NG * NCH, NPART, G * BPC, P], BF16, kind="Internal").ap()

        x_dram = x_in[0].rearrange("(b p) d -> p b d", p=P)
        out_dram = out[0].rearrange("(b p) d -> p b d", p=P)

        def setup():
            local = ExitStack()
            with local:
                wr_in = sb("wr_in", [E, D], where=local)
                aw_in = sb("aw_in", [P, 3, D], where=local)
                fw1_in = sb("fw1_in", [P, HT, D], where=local)
                fw2_in = sb("fw2_in", [P, HID], where=local)
                b1_in = sb("b1_in", [E, HID], where=local)
                b1_rest = sb("b1_rest", [E, HID], where=local)
                b1_rest2 = sb("b1_rest2", [E, HID], where=local)
                b1_split = sb("b1_split", [E, NPART, HID], BF16, where=local)
                abs_sum = sb("abs_sum", [P, 2], where=local)
                half_gamma = sb("half_gamma", [P, 2, 2], where=local)
                below = sb("below", [P, 2, HID], where=local)
                tern = sb("tern", [P, 2, HID], where=local)
                gam_in = sb("gam_in", [P, D], where=local)
                bet_in = sb("bet_in", [P, D], where=local)
                fb2_in = sb("fb2_in", [P, D], where=local)
                col_in = sb("col_in", [2 + HT, D], where=local)

                loaded = sem("loaded")
                small_loaded = sem("small_loaded")
                masks = sem("masks")
                masks_done = sem("masks_done")
                split_moved = sem("split_moved")
                split_ready = sem("split_ready")
                sums_ready = sem("sums_ready")
                total_ready = sem("total_ready")
                tern_ready = sem("tern_ready")
                transposed = sem("transposed")

                block = nc.Block()
                blk = block.__enter__()

                def row(ap):
                    n = ap.shape[0]
                    return bass.AP(tensor=ap.tensor, offset=ap.offset, ap=[[0, P], [1, n]])

                @blk.sync
                def _(sp):
                    for dst, src in ((x_res[:, :, :], x_dram), (wr_in[:, :], wr),
                                     (fw1_in[:, :, :], fw1.rearrange("(t p) d -> p t d", p=P)),
                                     (fw2_in[:, :], fw2), (aw_in[:, :, :], aw.rearrange("(t p) d -> p t d", p=P)),
                                     (b1_in[:, :], b1), (gam_in[:, :], row(gamma)), (bet_in[:, :], row(beta)),
                                     (fb2_in[:, :], row(fb2))):
                        sp.dma_start(dst, src).then_inc(loaded, 16)
                    sp.wait_ge(split_ready, 1)
                    for r in range(NPART):
                        sp.dma_start(b1_parts[r * E:(r + 1) * E, :], b1_split[:, r, :]).then_inc(split_moved, 16)
                    sp.wait_ge(split_moved, 16 * NPART)
                    sp.wait_ge(loaded, 16 * 9)

                @blk.scalar
                def _(act):
                    for dst, src in ((w_qkv0[:, 0, :], wq), (w_qkv0[:, 1, :], wk), (w_qkv0[:, 2, :], wv),
                                     (wo_sb[:, :], wo), (w1_sb[:, :, :], w1.rearrange("e d i -> d e i")),
                                     (wo2_sb[:, :, :], wo2.rearrange("(t p) d -> p t d", p=P)),
                                     (bo_bc[:, :], row(bo)), (bo2_bc[:, :], row(bo2)),
                                     (bv_bc[:, :], row(ab[2 * D:3 * D])),
                                     (col_in[0:2, :], ab[0:2 * D].rearrange("(t p) -> t p", p=P)),
                                     (col_in[2:2 + HT, :], fb1.rearrange("(t p) -> t p", p=P))):
                        act.dma_start(dst, src).then_inc(small_loaded, 16)
                    act.wait_ge(small_loaded, 16 * 11)

                @blk.gpsimd
                def _(pool):
                    pool.memset(ident[:, :], 0.0).then_inc(masks, 1)
                    pool.memset(ident_bf[:, :], 0.0).then_inc(masks, 1)
                    pool.memset(causal_add[:, :], 0.0).then_inc(masks, 1)
                    pool.memset(later_keys[:, :], 0.0).then_inc(masks, 1)
                    pool.memset(ones_mat[:, :], 1.0).then_inc(masks_done, 1)
                    pool.wait_ge(masks, 4)
                    pool.affine_select(out=ident[:, :], in_=ident[:, :], compare_op=ALU.not_equal, fill=1.0,
                                       base=0, pattern=[[-1, P]], channel_multiplier=1).then_inc(masks_done, 1)
                    pool.affine_select(out=ident_bf[:, :], in_=ident_bf[:, :], compare_op=ALU.not_equal, fill=1.0,
                                       base=0, pattern=[[-1, P]], channel_multiplier=1).then_inc(masks_done, 1)
                    pool.affine_select(out=causal_add[:, CH - P:CH], in_=causal_add[:, CH - P:CH],
                                       compare_op=ALU.is_ge, fill=NEG, base=0, pattern=[[-1, P]],
                                       channel_multiplier=1).then_inc(masks_done, 1)
                    pool.affine_select(out=later_keys[:, :], in_=later_keys[:, :], compare_op=ALU.is_ge, fill=NEG,
                                       base=0, pattern=[[1, P]], channel_multiplier=-1).then_inc(masks_done, 1)
                    pool.iota(rank[:, :], pattern=[[-1, E]], base=E, channel_multiplier=0,
                              allow_small_or_imprecise_dtypes=True).then_inc(masks_done, 1)

                @blk.vector
                def _(dve):
                    own = dve_chain.on(dve)
                    own(dve.memset(v_aug[:, :, :, DH:DH + 1], 1.0))
                    dve.wait_ge(loaded, 16 * 9)
                    dve.tensor_reduce(abs_sum[:, 0:1], fw1_in[:, :, :], axis=AX.XY, op=ALU.add,
                                      apply_absolute_value=True).then_inc(sums_ready, 1)
                    dve.tensor_reduce(abs_sum[:, 1:2], fw2_in[:, :], axis=AX.X, op=ALU.add,
                                      apply_absolute_value=True).then_inc(sums_ready, 1)
                    own(dve.tensor_copy(b1_split[:, 0, :], b1_in[:, :]))
                    own.wait()
                    own(dve.tensor_tensor(b1_rest[:, :], b1_in[:, :], b1_split[:, 0, :], ALU.subtract))
                    own.wait()
                    own(dve.tensor_copy(b1_split[:, 1, :], b1_rest[:, :]))
                    own.wait()
                    dve.tensor_tensor(b1_split[:, 2, :], b1_rest[:, :], b1_split[:, 1, :],
                                      ALU.subtract).then_inc(split_ready, 1)
                    dve.tensor_scalar(gamma_half[:, :], gam_in[:, :], 0.5, None, ALU.mult)
                    dve.tensor_scalar(beta_half[:, :], bet_in[:, :], 0.5, None, ALU.mult)
                    dve.tensor_scalar(fb2_half[:, :], fb2_in[:, :], 0.5, None, ALU.mult)
                    dve.wait_ge(total_ready, 1)
                    for s, sign in ((0, 0.5), (1, -0.5)):
                        own(dve.tensor_scalar(half_gamma[:, s, :], psum[:, 0, 0:2], 1.0 / (HID * D), 1e-5,
                                              ALU.mult, ALU.add))
                        own.wait()
                        own(dve.tensor_scalar(half_gamma[:, s, :], half_gamma[:, s, :], sign, None, ALU.mult))
                    own.wait()
                    fw1_flat = fw1_in[:, :, :].rearrange("p t d -> p (t d)")
                    for m, src in ((0, fw1_flat), (1, fw2_in[:, :])):
                        own(dve.tensor_scalar(below[:, m, :], src, half_gamma[:, 1, m:m + 1], None, ALU.is_lt))
                        own.wait()
                        dve.scalar_tensor_tensor(out=tern[:, m, :], in0=src, scalar=half_gamma[:, 0, m:m + 1],
                                                 in1=below[:, m, :], op0=ALU.is_gt,
                                                 op1=ALU.subtract).then_inc(tern_ready, 1)
                    dve.wait_ge(transposed, 1)
                    dve.tensor_copy(tw1_t[:, :, :], psum[:, 1, :].rearrange("p (t f) -> p t f", t=HT))
                    dve.tensor_copy(tw2_t[:, :, :], psum[:, 2, :].rearrange("p (t d) -> p t d", t=HT))
                    dve.tensor_copy(w_qkv1[:, :, :], psum[:, 3, 0:3 * D].rearrange("p (t d) -> p t d", t=3))
                    dve.tensor_copy(wr_t[:, :], psum[:, 4, 0:E])
                    dve.tensor_copy(bias_cols[:, :], psum[:, 5, 0:2 + HT])

                @blk.tensor
                def _(pe):
                    pe.wait_ge(masks_done, 6)
                    pe.wait_ge(sums_ready, 2)
                    pe.matmul(psum[:, 0, 0:2], ones_mat[:, :], abs_sum[:, :], start=True,
                              stop=True).then_inc(total_ready, 1)
                    pe.wait_ge(loaded, 16 * 9)
                    for t in range(3):
                        pe.transpose(psum[:, 3, t * P:(t + 1) * P], aw_in[:, t, :], ident[:, :])
                    pe.transpose(psum[:, 4, 0:E], wr_in[:, :], ident[0:E, 0:E])
                    pe.wait_ge(small_loaded, 16 * 11)
                    pe.transpose(psum[:, 5, 0:2 + HT], col_in[:, :], ident[0:2 + HT, 0:2 + HT])
                    pe.wait_ge(tern_ready, 2)
                    for t in range(HT):
                        pe.transpose(psum[:, 1, t * P:(t + 1) * P], tern[:, 0, t * D:(t + 1) * D], ident[:, :])
                    for t in range(HT):
                        last = pe.transpose(psum[:, 2, t * P:(t + 1) * P], tern[:, 1, t * P:(t + 1) * P], ident[:, :])
                    last.then_inc(transposed, 1)

                block.__exit__(None, None, None)

        class NormScratch:
            def __init__(self, where):
                self.stats = sb("ln_stats", [P, NB, 6], where=where)
                self.mean_var = sb("ln_mean_var", [P, NB, 2], where=where)
                self.v = sb("ln_v", [P, NB], where=where)
                self.rstd = sb("ln_rstd", [P, NB], where=where)
                self.tmp = sb("ln_tmp", [P, NB], where=where)

        def norm_stats(dve, own, s, src, b0, n):
            for b in range(b0, b0 + n):
                own(dve.bn_stats(s.stats[:, b, :], src[:, b, :]))
            own.wait()
            for b in range(b0, b0 + n):
                own(dve.bn_aggr(s.mean_var[:, b, :], s.stats[:, b, :]))
            own.wait()

        def norm_rstd(dve, own, s, eps, b0, n):
            v, r, t = s.v[:, b0:b0 + n], s.rstd[:, b0:b0 + n], s.tmp[:, b0:b0 + n]
            own(dve.tensor_scalar(v, s.mean_var[:, b0:b0 + n, 1], eps, None, ALU.add))
            own.wait()
            own(dve.tensor_scalar(t.bitcast(I32), v.bitcast(I32), 1, None, ALU.arith_shift_right))
            own.wait()
            own(dve.tensor_scalar(r.bitcast(I32), t.bitcast(I32), -1.0, float(0x5F3759DF), ALU.mult, ALU.add))
            own.wait()
            for _ in range(3):
                own(dve.tensor_tensor(t, r, r, ALU.mult))
                own.wait()
                own(dve.tensor_tensor(t, t, v, ALU.mult))
                own.wait()
                own(dve.tensor_scalar(t, t, -0.5, 1.5, ALU.mult, ALU.add))
                own.wait()
                own(dve.tensor_tensor(r, r, t, ALU.mult))
                own.wait()

        def norm_apply(dve, s, dst, src, b):
            return dve.tensor_scalar(dst[:, b, :], src[:, b, :], s.mean_var[:, b, 0:1], s.rstd[:, b:b + 1],
                                     ALU.subtract, ALU.mult)

        def bcast_blocks(tile2d, n):
            return tile2d[:, :].rearrange("p (a d) -> p a d", a=1).broadcast_to([P, n, D])

        def expert_layer(first):
            local = ExitStack()
            with local:
                s1, s2 = NormScratch(local), NormScratch(local)
                xn = sb("xn", [P, NB, D], where=local)
                xn_t = sb("xn_t", [P, T], where=local)
                xn_bias = sb("xn_bias", [P, NB, D], where=local)
                logit = sb("logit", [P, NB, E], where=local)
                top = sb("top", [P, NB], where=local)
                tied = sb("tied", [P, NB, E], where=local)
                onehot = sb("onehot", [P, NB, NPART * E], BF16, where=local)
                onehot_t = sb("onehot_t", [NPART * E, T], BF16, where=local)
                NX = 4
                x_mask = sb("x_mask", [P, NX, CH], where=local)
                h_t = sb("h_t", [P, 2, HT, CH], where=local)
                y = xn_bias

                xn_ready, xnt_psum, xnt_ready = sem("xn_ready"), sem("xnt_psum"), sem("xnt_ready")
                logits_done, onehot_ready = sem("logits_done"), sem("onehot_ready")
                oht_psum, oht_ready = sem("oht_psum"), sem("oht_ready")
                mask_psum, xmask_ready, experts_done = sem("mask_psum"), sem("xmask_ready"), sem("experts_done")
                gelu_done, down_done, y_ready = sem("gelu_done"), sem("down_done"), sem("y_ready")
                pool_pre, expert_mm, slots_set = sem("pool_pre"), sem("expert_mm"), sem("slots_set")
                block = nc.Block()
                blk = block.__enter__()

                @blk.tensor
                def _(pe):
                    for n in range(NCH):
                        pe.wait_ge(xn_ready, BPC * (n + 1))
                        for i in range(BPC):
                            last = pe.transpose(psum[:, n, i * P:(i + 1) * P], xn[:, n * BPC + i, :], ident[:, :])
                        last.then_inc(xnt_psum, 1)
                    for n in range(NCH):
                        pe.wait_ge(xnt_ready, n + 1)
                        for i in range(BPC):
                            b = n * BPC + i
                            last = pe.matmul(psum[:, 4, b * E:(b + 1) * E], xn_t[:, b * P:(b + 1) * P], wr_t[:, :],
                                             start=True, stop=True)
                    last.then_inc(logits_done, 1)
                    pe.wait_ge(onehot_ready, NPART)
                    for n in range(NCH):
                        if n >= 2:
                            pe.wait_ge(oht_ready, n - 1)
                        bank = psum[0:NPART * E, 5 + n % 2, 0:CH // 2].bitcast(BF16)
                        for i in range(BPC):
                            last = pe.transpose(bank[:, i * P:(i + 1) * P], onehot[:, n * BPC + i, :], ident_bf[:, :])
                        last.then_inc(oht_psum, 1)

                    def masks_of(k):
                        n, e = divmod(k, E)
                        if k >= 2:
                            pe.wait_ge(xmask_ready, k - 1)
                        elif k == 0:
                            pe.wait_ge(oht_ready, NCH)
                        for i in range(BPC):
                            b = n * BPC + i
                            last = pe.matmul(psum[:, 4 + k % 2, i * P:(i + 1) * P],
                                             onehot[:, b, e:e + 1].broadcast_to([P, P]), ident_bf[:, :],
                                             start=True, stop=True)
                        last.then_inc(mask_psum, 1)

                    def down(n):
                        pe.wait_ge(gelu_done, HT * (n + 1))
                        if n >= 2:
                            pe.wait_ge(y_ready, n - 1)
                        for i in range(BPC):
                            for t in range(HT):
                                last = pe.matmul(psum[:, 6 + n % 2, i * D:(i + 1) * D],
                                                 h_t[:, n % 2, t, i * P:(i + 1) * P], wo2_sb[:, t, :],
                                                 start=(t == 0), stop=(t == HT - 1))
                        last.then_inc(down_done, 1)

                    masks_of(0)
                    for n in range(NCH):
                        for e in range(E):
                            k = n * E + e
                            if k + 1 < NCH * E:
                                masks_of(k + 1)
                            pe.wait_ge(xmask_ready, k + 1)
                            if e == 0 and n >= 1:
                                pe.wait_ge(gelu_done, HT * n)
                            for t in range(HT):
                                last = pe.matmul(psum[:, t, :], w1_sb[:, e, t * P:(t + 1) * P], x_mask[:, k % NX, :],
                                                 start=(e == 0), stop=False)
                            last.then_inc(expert_mm, 1)
                            if e == 1 and n >= 1:
                                down(n - 1)
                        for t in range(HT):
                            pe.matmul(psum[:, t, :], b1_parts[:, t * P:(t + 1) * P], onehot_t[:, n * CH:(n + 1) * CH],
                                      start=False, stop=True).then_inc(experts_done, 1)
                    down(NCH - 1)

                @blk.scalar
                def _(act):
                    for n in range(NCH):
                        act.wait_ge(xnt_psum, n + 1)
                        act.copy(xn_t[:, n * CH:(n + 1) * CH], psum[:, n, :]).then_inc(xnt_ready, 1)
                    for n in range(NCH):
                        act.wait_ge(oht_psum, n + 1)
                        act.copy(onehot_t[:, n * CH:(n + 1) * CH],
                                 psum[0:NPART * E, 5 + n % 2, 0:CH // 2].bitcast(BF16)).then_inc(oht_ready, 1)
                    for n in range(NCH):
                        for t in range(HT):
                            act.wait_ge(experts_done, n * HT + t + 1)
                            if n >= 2:
                                act.wait_ge(down_done, n - 1)
                            act.activation(h_t[:, n % 2, t, :], psum[:, t, :], ACT.Gelu).then_inc(gelu_done, 1)

                @blk.gpsimd
                def _(pool):
                    if first:
                        pool.memset(k_slots[:, :, :].rearrange("p h t -> p (h t)").bitcast(I32), 0).then_inc(slots_set, 1)
                        for n in range(2):
                            pool.wait_ge(slots_set, 1 + n)
                            lo = SLOT * n + 32
                            pool.memset(k_slots[lo:lo + 32, n::2, :], 1.0).then_inc(slots_set, 1)
                        pool.wait_ge(slots_set, 3)
                    for n in range(NCH):
                        lo, hi = n * BPC, (n + 1) * BPC
                        pool.wait_ge(xn_ready, BPC * (n + 1))
                        pool.tensor_tensor(xn_bias[:, lo:hi, :], xn[:, lo:hi, :], bcast_blocks(bo2_bc, BPC),
                                           ALU.add).then_inc(pool_pre, 1)
                        pool.tensor_tensor(x_res[:, lo:hi, :], x_res[:, lo:hi, :], bcast_blocks(beta_half, BPC),
                                           ALU.add).then_inc(pool_pre, 1)

                @blk.vector
                def _(dve):
                    own = dve_chain.on(dve)
                    norm_stats(dve, own, s1, x_res, 0, NB)
                    norm_rstd(dve, own, s1, 1e-5, 0, NB)
                    for b in range(NB):
                        norm_apply(dve, s1, xn, x_res, b).then_inc(xn_ready, 1)
                    dve.wait_ge(logits_done, 1)
                    own(dve.tensor_copy(logit[:, :, :], psum[:, 4, 0:NB * E].rearrange("p (b e) -> p b e", e=E)))
                    own.wait()

                    def per_block(ap):
                        return ap.rearrange("p (b a) -> p b a", a=1).broadcast_to([P, NB, E])

                    own(dve.tensor_reduce(top[:, :], logit[:, :, :], axis=AX.X, op=ALU.max))
                    own.wait()
                    own(dve.tensor_tensor(tied[:, :, :], logit[:, :, :], per_block(top[:, :]), ALU.is_ge))
                    own.wait()
                    rank_b = rank[:, :].rearrange("p (a e) -> p a e", a=1).broadcast_to([P, NB, E])
                    own(dve.tensor_tensor(tied[:, :, :], tied[:, :, :], rank_b, ALU.mult))
                    own.wait()
                    own(dve.tensor_reduce(top[:, :], tied[:, :, :], axis=AX.X, op=ALU.max))
                    own.wait()
                    for r in range(NPART):
                        dve.tensor_tensor(onehot[:, :, r * E:(r + 1) * E], tied[:, :, :], per_block(top[:, :]),
                                          ALU.is_equal).then_inc(onehot_ready, 1)

                    def finish(n):
                        lo, hi = n * BPC, (n + 1) * BPC
                        dve.wait_ge(down_done, n + 1)
                        dve.wait_ge(pool_pre, 2 * NCH)
                        dve.tensor_tensor(y[:, lo:hi, :], psum[:, 6 + n % 2, :].rearrange("p (b d) -> p b d", d=D),
                                          xn_bias[:, lo:hi, :], ALU.add).then_inc(y_ready, 1)
                        dve.wait_ge(y_ready, n + 1)
                        norm_stats(dve, own, s2, y, lo, BPC)
                        norm_rstd(dve, own, s2, 1e-12, lo, BPC)
                        for b in range(lo, hi):
                            own(norm_apply(dve, s2, xn, y, b))
                        own.wait()
                        own(dve.tensor_tensor(y[:, lo:hi, :], xn[:, lo:hi, :], bcast_blocks(gamma_half, BPC), ALU.mult))
                        own.wait()
                        own(dve.tensor_tensor(x_res[:, lo:hi, :], y[:, lo:hi, :], x_res[:, lo:hi, :], ALU.add))

                    for k in range(NCH * E):
                        n = k // E
                        dve.wait_ge(mask_psum, k + 1)
                        if k >= NX:
                            dve.wait_ge(expert_mm, k - NX + 1)
                        dve.tensor_tensor(x_mask[:, k % NX, :], psum[:, 4 + k % 2, :], xn_t[:, n * CH:(n + 1) * CH],
                                          ALU.mult).then_inc(xmask_ready, 1)
                        if k % E == 4 and n >= 1:
                            finish(n - 1)
                    finish(NCH - 1)

                block.__exit__(None, None, None)

        def ternary_layer(last_layer):
            local = ExitStack()
            with local:
                s1 = NormScratch(local)
                xn = sb("xn", [P, NB, D], where=local)
                xn_t = sb("xn_t", [P, T], where=local)
                x_bias = sb("x_bias", [P, NB, D], where=local)
                h_t = sb("h_t", [P, 2, HT, CH], where=local)
                xn_ready, xnt_psum, xnt_ready = sem("xn_ready"), sem("xnt_psum"), sem("xnt_ready")
                up_done, relu_done, down_done = sem("up_done"), sem("relu_done"), sem("down_done")
                pool_pre, x_ready, stored = sem("pool_pre"), sem("x_ready"), sem("stored")
                block = nc.Block()
                blk = block.__enter__()

                @blk.tensor
                def _(pe):
                    def features(n):
                        pe.wait_ge(xn_ready, BPC * (n + 1))
                        if n >= 1:
                            pe.wait_ge(xnt_ready, n)
                        for i in range(BPC):
                            last = pe.transpose(psum[:, 4, i * P:(i + 1) * P], xn[:, n * BPC + i, :], ident[:, :])
                        last.then_inc(xnt_psum, 1)

                    def down(n):
                        if n >= 2:
                            pe.wait_ge(x_ready, n - 1)
                        pe.wait_ge(relu_done, HT * (n + 1))
                        for i in range(BPC):
                            for t in range(HT):
                                last = pe.matmul(psum[:, 6 + n % 2, i * D:(i + 1) * D],
                                                 h_t[:, n % 2, t, i * P:(i + 1) * P], tw2_t[:, t, :],
                                                 start=(t == 0), stop=(t == HT - 1))
                        last.then_inc(down_done, 1)

                    features(0)
                    for n in range(NCH):
                        pe.wait_ge(xnt_ready, n + 1)
                        for t in range(HT):
                            if n >= 1:
                                pe.wait_ge(relu_done, HT * (n - 1) + t + 1)
                            pe.matmul(psum[:, t, :], tw1_t[:, t, :], xn_t[:, n * CH:(n + 1) * CH],
                                      start=True, stop=True).then_inc(up_done, 1)
                        if n + 1 < NCH:
                            features(n + 1)
                        if n >= 1:
                            down(n - 1)
                    down(NCH - 1)

                @blk.scalar
                def _(act):
                    for n in range(NCH):
                        act.wait_ge(xnt_psum, n + 1)
                        act.copy(xn_t[:, n * CH:(n + 1) * CH], psum[:, 4, :]).then_inc(xnt_ready, 1)
                        for t in range(HT):
                            act.wait_ge(up_done, n * HT + t + 1)
                            if n >= 2:
                                act.wait_ge(down_done, n - 1)
                            act.activation(h_t[:, n % 2, t, :], psum[:, t, :], ACT.Relu,
                                           bias=fb1_col[:, t:t + 1]).then_inc(relu_done, 1)

                @blk.gpsimd
                def _(pool):
                    for n in range(NCH):
                        lo, hi = n * BPC, (n + 1) * BPC
                        pool.tensor_tensor(x_bias[:, lo:hi, :], x_res[:, lo:hi, :], bcast_blocks(fb2_half, BPC),
                                           ALU.add).then_inc(pool_pre, 1)

                @blk.vector
                def _(dve):
                    own = dve_chain.on(dve)
                    norm_stats(dve, own, s1, x_res, 0, NB)
                    norm_rstd(dve, own, s1, 1e-5, 0, NB)
                    for b in range(NB):
                        norm_apply(dve, s1, xn, x_res, b).then_inc(xn_ready, 1)
                    dve.wait_ge(xn_ready, NB)
                    dve.wait_ge(pool_pre, NCH)
                    for n in range(NCH):
                        lo, hi = n * BPC, (n + 1) * BPC
                        dve.wait_ge(down_done, n + 1)
                        dve.scalar_tensor_tensor(out=x_res[:, lo:hi, :].rearrange("p b d -> p (b d)"),
                                                 in0=psum[:, 6 + n % 2, :], scalar=0.5,
                                                 in1=x_bias[:, lo:hi, :].rearrange("p b d -> p (b d)"),
                                                 op0=ALU.mult, op1=ALU.add).then_inc(x_ready, 1)

                @blk.sync
                def _(sp):
                    if last_layer:
                        for n in range(NCH):
                            lo, hi = n * BPC, (n + 1) * BPC
                            sp.wait_ge(x_ready, n + 1)
                            sp.dma_start(out_dram[:, lo:hi, :], x_res[:, lo:hi, :]).then_inc(stored, 16)
                        sp.wait_ge(stored, 16 * NCH)

                block.__exit__(None, None, None)

        HALF = NG // 2
        STEPS = [(g, c) for c in range(NCH) for g in range(HALF)] + \
                [(g, c) for c in reversed(range(NCH)) for g in range(HALF, NG)]
        AHEAD = 2

        def quads_of(step):
            return [(step, j) for j in range(BPC * (step[1] + 1))]

        def max_units_of(step):
            return [(step, i, kc, h) for i in range(BPC) for kc in range(step[1] + 1) for h in range(G)]

        def units_beside_quads():
            deadlines, quads, units = [], 0, 0
            for n, s in enumerate(STEPS):
                if n >= AHEAD:
                    units += len(max_units_of(s))
                    deadlines.append((quads - 3, units))
                quads += len(quads_of(s))
            counts, done = [], 0
            for t in range(quads):
                pace = max([(u - done) / (q - t) for q, u in deadlines if q > t], default=0)
                counts.append(min(units - done, int(pace + 0.999)))
                done += counts[-1]
            return counts

        TURNS = [t for s in STEPS[:AHEAD] for t in ((None, max_units_of(s)), (None, []))]
        units_left = [u for s in STEPS[AHEAD:] for u in max_units_of(s)]
        for q, count in zip([q for s in STEPS for q in quads_of(s)], units_beside_quads()):
            TURNS.append((q, units_left[:count]))
            units_left = units_left[count:]
        assert not units_left
        TURNS += [(None, [])] * 3

        def attention_layer(w_qkv, biased, projected):
            local = ExitStack()
            with local:
                s1 = NormScratch(local)
                xn = sb("xn", [P, NB, D], where=local)
                ctx = xn
                xn_t = sb("xn_t", [P, T], where=local)
                NP = 4
                probs = sb("probs", [P, NP, 2, CH], where=local)
                qf = sb("qf", [P, 2, CH], where=local)
                rest = sb("rest", [P, 2, CH], where=local)
                qk_parts = sb("qk_parts", [P, 2, NPART, CH], BF16, where=local)
                out_t = sb("out_t", [P, 2, CH], where=local)
                recip = sb("recip", [P, 2, BPC, G], where=local)
                junk = sb("junk", [P, 2, CH], BF16, where=local)
                part_max = sb("part_max", [P, 2, G, BPC, NCH], where=local)
                neg_max = sb("neg_max", [P, 2, G * BPC], where=local)
                nm_rest = sb("nm_rest", [G * BPC, P], where=local)
                nm_parts = sb("nm_parts", [G * BPC, 2, NPART, P], BF16, where=local)

                xn_ready, xnt_psum, xnt_ready = sem("xn_ready"), sem("xnt_psum"), sem("xnt_ready")
                proj_done, qf_ready, hi_ready, rest_ready = sem("proj_done"), sem("qf_ready"), sem("hi_ready"), sem("rest_ready")
                mid_ready, lo_ready, v_psum, v_ready = sem("mid_ready"), sem("lo_ready"), sem("v_psum"), sem("v_ready")
                parts_stored = [sem(f"parts_stored{i}") for i in range(2)]
                slots_landed = [sem(f"slots_landed{g}") for g in range(2)]
                q_zeroed = sem("q_zeroed")
                block = nc.Block()
                blk = block.__enter__()

                PROJ = [(n, m) for n in range(NCH) for m in range(2)]


                ring_read, ring_full, o_bank_set = sem("ring_read"), sem("ring_full"), sem("o_bank_set")
                negmax_ready, negmax_split = sem("negmax_ready"), sem("negmax_split")
                negmax_stored = [sem(f"negmax_stored{i}") for i in range(2)]
                negmax_landed = [sem(f"negmax_landed{i}") for i in range(4)]
                scores_done, exp_done, pv_done = sem("scores_done"), sem("exp_done"), sem("pv_done")
                out_copied = sem("out_copied")
                S_BANKS, O_BANK, RING_BANKS, RING = 0, 4, 5, 3

                step_no = {s: i for i, s in enumerate(STEPS)}
                quad_no = {q: i for i, q in enumerate(q for q, _ in TURNS if q)}
                diagonal = {q for q in quad_no if q[1] >= BPC * q[0][1]}

                def first_query(q):
                    (_, c), j = q
                    return max(0, j - BPC * c) * P

                def late_work():
                    plan, ended_m, ended_q = [], [], []
                    for q, units in TURNS:
                        m_now = [u[0] for u in units if u == max_units_of(u[0])[-1]]
                        q_now = [q[0]] if q and q[1] == BPC * (q[0][1] + 1) - 1 else []
                        plan.append((m_now, ended_m[-1] if ended_m else [], ended_q[-1] if ended_q else [],
                                     ended_q[-2] if len(ended_q) > 1 else []))
                        ended_m.append(m_now)
                        ended_q.append(q_now)
                    return plan

                PLAN = late_work()

                RING_ITEMS, ring_no = [], {}
                for (_, units), (_, turn_max, _, turn_out) in zip(TURNS, PLAN):
                    RING_ITEMS.append([("scores", u) for u in units] + [("max", s) for s in turn_max] +
                                      [("out", s) for s in turn_out])
                    for item in RING_ITEMS[-1]:
                        ring_no[item] = len(ring_no)
                last_unit = {s: max(n for item, n in ring_no.items() if item[0] == "scores" and item[1][0] == s)
                             for s in STEPS}

                @blk.tensor
                def _(pe):
                    for n in range(NCH):
                        pe.wait_ge(xn_ready, BPC * (n + 1))
                        if n >= 2:
                            pe.wait_ge(xnt_ready, n - 1)
                        for i in range(BPC):
                            last = pe.transpose(psum[:, n % 2, i * P:(i + 1) * P], xn[:, n * BPC + i, :], ident[:, :])
                        last.then_inc(xnt_psum, 1)
                        pe.wait_ge(xnt_ready, n + 1)
                        for m in range(2):
                            k = 2 * n + m
                            if k >= 4:
                                pe.wait_ge(qf_ready, k - 3)
                            pe.matmul(psum[:, 2 + k % 4, :], w_qkv[:, m, :], xn_t[:, n * CH:(n + 1) * CH],
                                      start=True, stop=True).then_inc(proj_done, 1)
                        if n >= 2:
                            pe.wait_ge(v_ready, n - 1)
                        for i in range(BPC):
                            b = n * BPC + i
                            last = pe.matmul(psum[:, 6 + n % 2, i * D:(i + 1) * D], xn_t[:, b * P:(b + 1) * P],
                                             w_qkv[:, 2, :], start=True, stop=True)
                        last.then_inc(v_psum, 1)
                    pe.wait_ge(qf_ready, len(PROJ))
                    pe.wait_ge(v_ready, NCH)

                    def score_tile(q, pr):
                        (g, c), j = q
                        n = quad_no[q]
                        off = first_query(q)
                        if j == 0 and pr == 0:
                            pe.wait_ge(negmax_landed[step_no[q[0]] % 4], 32 * (step_no[q[0]] // 4 + 1))
                        tile = 2 * n + pr
                        if tile >= 2:
                            pe.wait_ge(exp_done, tile - 1)
                        for par in range(2):
                            last = pe.matmul(psum[:, S_BANKS + 2 * (tile % 2) + par, off:CH],
                                             k_slots[:, G * g + 2 * pr + par, j * P:(j + 1) * P],
                                             q_slots[:, 2 * g + pr, c * CH + off:(c + 1) * CH],
                                             start=True, stop=q not in diagonal)
                        if q in diagonal:
                            for par in range(2):
                                last = pe.matmul(psum[:, S_BANKS + 2 * (tile % 2) + par, off:off + P],
                                                 ident_bf[:, :], later_keys[:, :], start=False, stop=True)
                        last.then_inc(scores_done, 1)

                    def values(q):
                        (g, c), j = q
                        n = quad_no[q]
                        off = first_query(q)
                        pe.wait_ge(exp_done, 2 * n + 2)
                        if j == 0:
                            pe.wait_ge(*((out_copied, step_no[q[0]]) if step_no[q[0]] else (o_bank_set, 1)))
                        for h in range(G):
                            last = pe.matmul(psum[VW * h:VW * h + DH + 1, O_BANK, off:CH],
                                             v_aug[:, j, G * g + h, :],
                                             probs[:, (2 * n + h // 2) % NP, h % 2, off:CH],
                                             start=(j == 0), stop=(j == BPC * (c + 1) - 1))
                        last.then_inc(pv_done, 1)

                    def ring_item(item):
                        kind, what = item
                        n = ring_no[item]
                        bank = RING_BANKS + n % RING
                        if n >= RING:
                            pe.wait_ge(ring_read, n - RING + 1)
                        if kind == "scores":
                            (g, c), i, kc, h = what
                            if (g, i, kc, h) == (0, 0, 0, 0):
                                pe.wait_ge(slots_landed[c % 2], 16 * 4 * (c // 2 + 1))
                            w = CH if kc < c else (i + 1) * P
                            qb = BPC * c + i
                            last = pe.matmul(psum[:, bank, 0:w], q_slots[:, 2 * g + h // 2, qb * P:(qb + 1) * P],
                                             k_slots[:, G * g + h, kc * CH:kc * CH + w], start=True, stop=True)
                        elif kind == "max":
                            k = step_no[what]
                            pe.wait_ge(negmax_ready, k + 1)
                            last = pe.transpose(psum[0:G * BPC, bank, 0:P], neg_max[:, k % 2, :], ident[:, :])
                        else:
                            k = step_no[what]
                            pe.wait_ge(out_copied, k + 1)
                            for i in range(BPC):
                                last = pe.transpose(psum[:, bank, i * P:(i + 1) * P],
                                                    out_t[:, k % 2, i * P:(i + 1) * P], ident[:, :])
                        last.then_inc(ring_full, 1)

                    previous = None
                    for (q, _), items in zip(TURNS, RING_ITEMS):
                        cuts = [0, len(items) // 4, len(items) // 2 + len(items) // 4, len(items)]
                        if q:
                            score_tile(q, 0)
                        for item in items[cuts[0]:cuts[1]]:
                            ring_item(item)
                        if q:
                            score_tile(q, 1)
                        for item in items[cuts[1]:cuts[2]]:
                            ring_item(item)
                        if previous:
                            values(previous)
                        for item in items[cuts[2]:cuts[3]]:
                            ring_item(item)
                        previous = q

                @blk.scalar
                def _(act):
                    for k, (n, m) in enumerate(PROJ):
                        if m == 0:
                            act.wait_ge(xnt_psum, n + 1)
                            act.copy(xn_t[:, n * CH:(n + 1) * CH], psum[:, n % 2, :]).then_inc(xnt_ready, 1)
                        act.wait_ge(proj_done, k + 1)
                        if k >= 2:
                            act.wait_ge(lo_ready, k - 1)
                            act.wait_ge(parts_stored[k % 2], 16 * sum(TERMS) * (k // 2))
                        if biased:
                            act.activation(qf[:, k % 2, :], psum[:, 2 + k % 4, :], ACT.Identity,
                                           bias=qk_bias[:, m:m + 1]).then_inc(qf_ready, 1)
                        else:
                            act.copy(qf[:, k % 2, :], psum[:, 2 + k % 4, :]).then_inc(qf_ready, 1)
                        act.wait_ge(qf_ready, k + 1)
                        act.copy(qk_parts[:, k % 2, 0, :], qf[:, k % 2, :]).then_inc(hi_ready, 1)
                        act.wait_ge(rest_ready, k + 1)
                        act.copy(qk_parts[:, k % 2, 1, :], rest[:, k % 2, :]).then_inc(mid_ready, 1)
                    for (q, _), (_, _, copy_out, _) in zip(TURNS, PLAN):
                        if q:
                            n = quad_no[q]
                            off = first_query(q)
                            for pr in range(2):
                                tile = 2 * n + pr
                                act.wait_ge(scores_done, tile + 1)
                                if tile >= NP:
                                    act.wait_ge(pv_done, (tile - NP) // 2 + 1)
                                bank = S_BANKS + 2 * (tile % 2)
                                act.activation(probs[:, tile % NP, :, off:CH], psum[:, bank:bank + 2, off:CH],
                                               ACT.Exp, scale=SCALE).then_inc(exp_done, 1)
                        for s in copy_out:
                            k = step_no[s]
                            last_quad = quad_no[(s, BPC * (s[1] + 1) - 1)]
                            act.wait_ge(pv_done, last_quad + 1)
                            if k >= 2:
                                act.wait_ge(ring_full, ring_no["out", STEPS[k - 2]] + 1)
                            act.copy(out_t[:, k % 2, :], psum[:, O_BANK, :]).then_inc(out_copied, 1)

                @blk.vector
                def _(dve):
                    own = dve_chain.on(dve)

                    def normalise(n):
                        norm_stats(dve, own, s1, x_res, n * BPC, BPC)
                        norm_rstd(dve, own, s1, 1e-5, n * BPC, BPC)
                        for b in range(n * BPC, (n + 1) * BPC):
                            norm_apply(dve, s1, xn, x_res, b).then_inc(xn_ready, 1)

                    def split(k):
                        dve.wait_ge(hi_ready, k + 1)
                        dve.tensor_tensor(rest[:, k % 2, :], qf[:, k % 2, :], qk_parts[:, k % 2, 0, :],
                                          ALU.subtract).then_inc(rest_ready, 1)
                        dve.wait_ge(mid_ready, k + 1)
                        dve.tensor_tensor(qk_parts[:, k % 2, 2, :], rest[:, k % 2, :], qk_parts[:, k % 2, 1, :],
                                          ALU.subtract).then_inc(lo_ready, 1)

                    def values_out(n):
                        dve.wait_ge(v_psum, n + 1)
                        dst = v_aug[:, n * BPC:(n + 1) * BPC, :, 0:DH]
                        src = psum[:, 6 + n % 2, :].rearrange("p (b h d) -> p b h d", h=H, d=DH)
                        if biased:
                            for i in range(BPC):
                                last = dve.tensor_tensor(dst[:, i], src[:, i],
                                                         bv_bc[:, :].rearrange("p (h d) -> p h d", d=DH), ALU.add)
                        else:
                            last = dve.tensor_copy(dst, src)
                        last.then_inc(v_ready, 1)

                    normalise(0)
                    for n in range(NCH):
                        if n + 1 < NCH:
                            normalise(n + 1)
                        split(2 * n)
                        split(2 * n + 1)
                        values_out(n)
                    dve.wait_ge(xnt_psum, NCH)
                    dve.wait_ge(qf_ready, len(PROJ))

                    junk_used = [0, 0]
                    dve.memset(psum[:, O_BANK, :], 0.0).then_inc(o_bank_set, 1)
                    for items, (m_now, _, _, _) in zip(RING_ITEMS, PLAN):
                        for item in items:
                            kind, what = item
                            n = ring_no[item]
                            bank = RING_BANKS + n % RING
                            dve.wait_ge(ring_full, n + 1)
                            if kind == "scores":
                                s, i, kc, h = what
                                dst = part_max[:, step_no[s] % 2, h, i, kc:kc + 1]
                                if kc < s[1]:
                                    dve.tensor_reduce(dst, psum[:, bank, :], axis=AX.X,
                                                      op=ALU.max).then_inc(ring_read, 1)
                                else:
                                    w = (i + 1) * P
                                    if junk_used[n % 2]:
                                        dve.wait_ge(ring_read, junk_used[n % 2])
                                    dve.tensor_tensor_reduce(out=junk[:, n % 2, 0:w], in0=psum[:, bank, 0:w],
                                                             in1=causal_add[:, CH - w:CH], scale=1.0,
                                                             scalar=-3.0e38, op0=ALU.add, op1=ALU.max,
                                                             accum_out=dst).then_inc(ring_read, 1)
                                    junk_used[n % 2] = n + 1
                            elif kind == "max":
                                k = step_no[what]
                                if k >= 2:
                                    dve.wait_ge(negmax_stored[k % 2], 16 * (k // 2))
                                src = psum[0:G * BPC, bank, 0:P]
                                own(dve.tensor_copy(nm_parts[:, k % 2, 0, :], src))
                                own.wait()
                                dve.tensor_tensor(nm_rest[:, :], src, nm_parts[:, k % 2, 0, :],
                                                  ALU.subtract).then_inc(ring_read, 1)
                                dve.wait_ge(ring_read, n + 1)
                                own(dve.tensor_copy(nm_parts[:, k % 2, 1, :], nm_rest[:, :]))
                                own.wait()
                                dve.tensor_tensor(nm_parts[:, k % 2, 2, :], nm_rest[:, :], nm_parts[:, k % 2, 1, :],
                                                  ALU.subtract).then_inc(negmax_split, 1)
                                dve.wait_ge(negmax_split, k + 1)
                            else:
                                (g, c), k = what, step_no[what]
                                rows = psum[:, bank, :].rearrange("p (b h w) -> p b h w", h=G, w=VW)
                                own(dve.reciprocal(recip[:, k % 2, :, :], rows[:, :, :, DH]))
                                own.wait()
                                r = recip[:, k % 2, :, :].rearrange("p b (h a) -> p b h a", a=1)
                                dst = ctx[:, c * BPC:(c + 1) * BPC, g * G * DH:(g + 1) * G * DH]
                                dve.tensor_tensor(dst.rearrange("p b (h d) -> p b h d", d=DH), rows[:, :, :, 0:DH],
                                                  r.broadcast_to([P, BPC, G, DH]), ALU.mult).then_inc(ring_read, 1)
                                dve.wait_ge(ring_read, n + 1)
                        for s in m_now:
                            k = step_no[s]
                            dve.wait_ge(ring_read, last_unit[s] + 1)
                            if k >= 2:
                                dve.wait_ge(ring_full, ring_no["max", STEPS[k - 2]] + 1)
                            dve.tensor_reduce(neg_max[:, k % 2, :],
                                              part_max[:, k % 2, :, :, 0:s[1] + 1].rearrange("p h i c -> p (h i) c"),
                                              axis=AX.X, op=ALU.max, negate=True).then_inc(negmax_ready, 1)

                @blk.gpsimd
                def _(pool):
                    for n in range(2):
                        lo = SLOT * n + 32
                        pool.memset(q_slots[lo:lo + 32, :, :].rearrange("p h t -> p (h t)").bitcast(I32), 0).then_inc(q_zeroed, 1)

                @blk.sync
                def _(sp):
                    sp.wait_ge(q_zeroed, 2)
                    for k, (n, m) in enumerate(PROJ):
                        sp.wait_ge(lo_ready, k + 1)
                        for i, r in enumerate(ROW_PARTS[m]):
                            sp.dma_start(slot_dram[m][:, i, :, n * CH:(n + 1) * CH],
                                         qk_parts[:, k % 2, r, :]).then_inc(parts_stored[k % 2], 16)
                        if m == 0:
                            continue
                        for i in range(2):
                            sp.wait_ge(parts_stored[i], 16 * sum(TERMS) * (n + 1))
                        if n >= 2:
                            sp.wait_ge(slots_landed[n % 2], 16 * 4 * (n // 2))
                        cols = slice(n * CH, (n + 1) * CH)
                        for par in range(2):
                            for mm, slots in enumerate((q_slots, k_slots[:, par::2, :])):
                                rows = slot_dram[mm].rearrange("(a two) i d t -> two (i d) a t", two=2)
                                sp.dma_start(slots[SLOT * par:SLOT * par + QK_ROWS, :, cols],
                                             rows[par, :, :, cols]).then_inc(slots_landed[n % 2], 16)
                    for k, (g, c) in enumerate(STEPS):
                        sp.wait_ge(negmax_split, k + 1)
                        sp.dma_start(negmax_dram[k].rearrange("r hi q -> hi r q"),
                                     nm_parts[:, k % 2, :, :]).then_inc(negmax_stored[k % 2], 16)
                        sp.wait_ge(negmax_stored[k % 2], 16 * (k // 2 + 1))
                        for par in range(2):
                            lo = SLOT * par + QK_ROWS
                            src = negmax_dram[k].rearrange("r (pr two i) q -> two r pr (i q)", pr=2, two=2)[par]
                            sp.dma_start(q_slots[lo:lo + NPART, 2 * g:2 * g + 2, c * CH:(c + 1) * CH],
                                         src).then_inc(negmax_landed[k % 4], 16)
                    for i in range(4):
                        sp.wait_ge(negmax_landed[i], 32 * len(STEPS[i::4]))

                block.__exit__(None, None, None)

                ct_psum, ct_ready, o_done = sem("ct_psum"), sem("ct_ready"), sem("o_done")
                block = nc.Block()
                blk = block.__enter__()

                if projected:
                    @blk.tensor
                    def _(pe):
                        for n in range(NCH):
                            for i in range(BPC):
                                last = pe.transpose(psum[:, n, i * P:(i + 1) * P], ctx[:, n * BPC + i, :], ident[:, :])
                            last.then_inc(ct_psum, 1)
                        for n in range(NCH):
                            pe.wait_ge(ct_ready, n + 1)
                            for i in range(BPC):
                                b = n * BPC + i
                                last = pe.matmul(psum[:, 4 + n, i * D:(i + 1) * D], xn_t[:, b * P:(b + 1) * P],
                                                 wo_sb[:, :], start=True, stop=True)
                            last.then_inc(o_done, 1)

                    @blk.scalar
                    def _(act):
                        for n in range(NCH):
                            act.wait_ge(ct_psum, n + 1)
                            act.copy(xn_t[:, n * CH:(n + 1) * CH], psum[:, n, :]).then_inc(ct_ready, 1)

                @blk.vector
                def _(dve):
                    own = dve_chain.on(dve)
                    for n in range(NCH):
                        lo, hi = n * BPC, (n + 1) * BPC
                        if projected:
                            own(dve.tensor_tensor(x_res[:, lo:hi, :], x_res[:, lo:hi, :], bcast_blocks(bo_bc, BPC), ALU.add))
                            own.wait()
                            dve.wait_ge(o_done, n + 1)
                            own(dve.tensor_tensor(x_res[:, lo:hi, :], psum[:, 4 + n, :].rearrange("p (b d) -> p b d", d=D),
                                                  x_res[:, lo:hi, :], ALU.add))
                        else:
                            own(dve.tensor_tensor(x_res[:, lo:hi, :], ctx[:, lo:hi, :], x_res[:, lo:hi, :], ALU.add))

                block.__exit__(None, None, None)

        setup()
        expert_layer(first=True)
        attention_layer(w_qkv0, biased=False, projected=True)
        expert_layer(first=False)
        ternary_layer(last_layer=False)
        attention_layer(w_qkv1, biased=True, projected=False)
        ternary_layer(last_layer=True)


_INS = ['L0_attn_x', 'L0_attn_wq', 'L0_attn_wk', 'L0_attn_wv', 'L0_attn_wo', 'L0_attn_bo', 'L0_ffn_Wr', 'L0_ffn_W1',
        'L0_ffn_b1', 'L0_ffn_Wo', 'L0_ffn_bo', 'L0_ffn_gamma', 'L0_ffn_beta', 'L1_attn_W', 'L1_attn_b', 'L1_ffn_W1',
        'L1_ffn_b1', 'L1_ffn_W2', 'L1_ffn_b2']
_OUT_SHAPE = (1, T, D)


def kernel(**inputs):
    import numpy as _np
    import concourse.bacc as _bacc
    from concourse import mybir as _mybir
    from concourse.bass_utils import run_bass_kernel_spmd as _run

    nc = _bacc.Bacc("TRN2", target_bir_lowering=False, num_devices=1)
    arrays, args = {}, []
    for name in _INS:
        a = _np.ascontiguousarray(inputs[name])
        arrays[f"in_{name}_dram"] = a
        args.append(nc.dram_tensor(f"in_{name}_dram", a.shape, _mybir.dt.from_np(a.dtype), kind="ExternalInput").ap())
    out = nc.dram_tensor("out_0_dram", _OUT_SHAPE, _mybir.dt.float32, kind="ExternalOutput").ap()
    macaron_layers(nc, *args, out)
    r = _run(nc, [arrays], core_ids=[0])
    return r.results[0]["out_0_dram"]
```

```python
from contextlib import ExitStack

import concourse.bass as bass
from concourse import mybir

F32 = mybir.dt.float32
BF16 = mybir.dt.bfloat16
F16 = mybir.dt.float16
I32 = mybir.dt.int32
ALU = mybir.AluOpType
ACT = mybir.ActivationFunctionType
AX = mybir.AxisListType

P = 128
T = 2048
D = 128
NB = T // P
CH = 512
NCH = T // CH
BPC = CH // P
H = 16
DH = D // H
G = 4
NG = H // G
SCALE = float(DH) ** -0.5
E = 8
HID = 512
HT = HID // P
X_SCALE = 4096.0
NEG = -1.0e30
NPART = 3
TERMS = 3
Q_PARTS, K_PARTS = (0, 1, 0), (0, 0, 1)
SLOT = 32
MAX_ROW = TERMS * DH
MAX_PARTS = 2
MAX_UNIT = 16384.0
VW = 32


class Chain:

    def __init__(self, semaphore):
        self.semaphore, self.count = semaphore, 0

    def on(self, engine):
        self.engine = engine
        return self

    def __call__(self, instruction):
        instruction.then_inc(self.semaphore, 1)
        self.count += 1
        return instruction

    def wait(self):
        if self.count:
            self.engine.wait_ge(self.semaphore, self.count)


def macaron_layers(nc, x_in, wq, wk, wv, wo, bo, wr, w1, b1, wo2, bo2, gamma, beta,
                   aw, ab, fw1, fb1, fw2, fb2, out):
    stack = ExitStack()
    names = [0]

    buffers = {}

    def sb(name, shape, dt=F32):
        if name not in buffers:
            buffers[name] = stack.enter_context(nc.sbuf_tensor(name, shape, dt))
        return buffers[name]

    def sem(name):
        names[0] += 1
        return stack.enter_context(nc.semaphore(f"{name}_{names[0]}"))

    with stack:
        blk = stack.enter_context(nc.Block())
        psum = stack.enter_context(nc.psum_tensor("psum", [P, 8, CH], F32))

        x_res = sb("x_res", [P, NB, D])
        ident = sb("ident", [P, P])
        ident_bf = sb("ident_bf", [P, P], BF16)
        causal_add = sb("causal_add", [P, CH])
        later_keys = sb("later_keys", [P, P], BF16)
        ones_mat = sb("ones_mat", [P, P])
        xn = sb("xn", [P, NB, D])
        xn_t = sb("xn_t", [P, T])
        hidden = sb("hidden", [P, 2, HT, CH])
        parts = sb("parts", [P, 8 * 2 * CH], F16)
        x_plus = sb("x_plus", [P, NB, D])
        q_slots = sb("q_slots", [P, NG, T], F16)
        k_slots = sb("k_slots", [P, H, T], F16)
        exp_scale = sb("exp_scale", [P, 2])
        v_aug = sb("v_aug", [P, NB, H, DH + 1])
        w_qkv0 = sb("w_qkv0", [P, 3, D])
        w_qkv1 = sb("w_qkv1", [P, 3, D])
        wo_sb = sb("wo_sb", [P, D])
        bo_bc = sb("bo_bc", [P, D])
        bv_bc = sb("bv_bc", [P, D])
        bias_cols = sb("bias_cols", [P, 2 + HT])
        qk_bias, fb1_col = bias_cols[:, 0:2], bias_cols[:, 2:2 + HT]
        wr_t = sb("wr_t", [P, E])
        w1_parts = sb("w1_parts", [P, E, 2, HID], F16)
        w1_scale = sb("w1_scale", [P, 1])
        unscale = sb("unscale", [P, 1])
        b1_parts = sb("b1_parts", [NPART * E, HID], BF16)
        wo2_sb = sb("wo2_sb", [P, HT, D])
        bo2_bc = sb("bo2_bc", [P, D])
        gamma_half = sb("gamma_half", [P, D])
        beta_half = sb("beta_half", [P, D])
        rank = sb("rank", [P, E])
        tw1_t = sb("tw1_t", [P, HT, P], F16)
        tw2_t = sb("tw2_t", [P, HT, D])
        fb2_half = sb("fb2_half", [P, D])

        dve_chain = Chain(sem("dve_own"))
        slot_dram = [nc.dram_tensor(f"{n}_rows", [H, TERMS + 1, DH, T], F16, kind="Internal").ap() for n in ("q", "k")]

        x_dram = x_in[0].rearrange("(b p) d -> p b d", p=P)
        out_dram = out[0].rearrange("(b p) d -> p b d", p=P)

        class NormScratch:
            def __init__(self, name):
                self.stats = sb(f"{name}_stats", [P, NB, 6])
                self.mean_var = sb(f"{name}_mean_var", [P, NB, 2])
                self.v = sb(f"{name}_v", [P, NB])
                self.rstd = sb(f"{name}_rstd", [P, NB])
                self.tmp = sb(f"{name}_tmp", [P, NB])

        def norm_stats(dve, own, s, src, b0, n):
            own.wait()
            for b in range(b0, b0 + n):
                own(dve.bn_stats(s.stats[:, b, :], src[:, b, :]))
            own.wait()
            for b in range(b0, b0 + n):
                own(dve.bn_aggr(s.mean_var[:, b, :], s.stats[:, b, :]))
            own.wait()

        def norm_rstd(dve, own, s, eps, b0, n):
            v, r, t = s.v[:, b0:b0 + n], s.rstd[:, b0:b0 + n], s.tmp[:, b0:b0 + n]
            own(dve.tensor_scalar(v, s.mean_var[:, b0:b0 + n, 1], eps, None, ALU.add))
            own.wait()
            own(dve.tensor_scalar(t.bitcast(I32), v.bitcast(I32), 1, None, ALU.arith_shift_right))
            own.wait()
            own(dve.tensor_scalar(r.bitcast(I32), t.bitcast(I32), -1.0, float(0x5F3759DF), ALU.mult, ALU.add))
            own.wait()
            for _ in range(3):
                own(dve.scalar_tensor_tensor(out=t, in0=r, scalar=-0.5, in1=r, op0=ALU.mult, op1=ALU.mult))
                own.wait()
                own(dve.tensor_tensor(t, t, v, ALU.mult))
                own.wait()
                own(dve.scalar_tensor_tensor(out=r, in0=t, scalar=1.5, in1=r, op0=ALU.add, op1=ALU.mult))
                own.wait()

        def norm_apply(dve, s, dst, src, b):
            return dve.tensor_scalar(dst[:, b, :], src[:, b, :], s.mean_var[:, b, 0:1], s.rstd[:, b:b + 1],
                                     ALU.subtract, ALU.mult)

        def bcast_blocks(tile2d, n):
            return tile2d[:, :].rearrange("p (a d) -> p a d", a=1).broadcast_to([P, n, D])

        class Norms:

            def __init__(self, name, order):
                self.ready, self.order = sem(name), order

            def wait(self, engine, chunk):
                engine.wait_ge(self.ready, BPC * (self.order.index(chunk) + 1))

            def make(self, dve, own, scratch, chunk):
                norm_stats(dve, own, scratch, x_res, chunk * BPC, BPC)
                norm_rstd(dve, own, scratch, 1e-5, chunk * BPC, BPC)
                for b in range(chunk * BPC, (chunk + 1) * BPC):
                    norm_apply(dve, scratch, xn, x_res, b).then_inc(self.ready, 1)

        class Projection:
            V_BANK = 3

            def __init__(self, w_qkv, biased, norms, order):
                self.w_qkv, self.biased, self.norms, self.order = w_qkv, biased, norms, order
                self.xnt_psum, self.xnt_ready = sem("xnt_psum"), sem("xnt_ready")
                self.proj_done, self.hi_ready, self.lo_ready = sem("proj_done"), sem("hi_ready"), sem("lo_ready")
                self.v_psum, self.v_ready = sem("v_psum"), sem("v_ready")

            def t_bank(self, n):
                return psum[:, 4 if n == 0 else 0, :]

            def qk_bank(self, n, m):
                return psum[:, (4 if n == 0 else 1) + m, :]

            def parts_of(self, n, m):
                if n == 0:
                    return hidden[:, 0, m, :].bitcast(F16).rearrange("p (r t) -> p r t", r=2)
                k = 2 * n + m
                return parts[:, 2 * k * CH:2 * (k + 1) * CH].rearrange("p (r t) -> p r t", r=2)

            def transposes(self, pe, n):
                self.norms.wait(pe, self.order[n])
                if n >= 2:
                    pe.wait_ge(self.xnt_ready, n)
                for i in range(BPC):
                    last = pe.transpose(self.t_bank(n)[:, i * P:(i + 1) * P], xn[:, self.order[n] * BPC + i, :], ident[:, :])
                last.then_inc(self.xnt_psum, 1)

            def queries_keys(self, pe, n):
                pe.wait_ge(self.xnt_ready, n + 1)
                for m in range(2):
                    if n >= 2:
                        pe.wait_ge(self.lo_ready, 2 * n + m - 1)
                    pe.matmul(self.qk_bank(n, m), self.w_qkv[:, m, :], xn_t[:, n * CH:(n + 1) * CH],
                              start=True, stop=True).then_inc(self.proj_done, 1)

            def values(self, pe, n):
                if n >= 1:
                    pe.wait_ge(self.v_ready, n)
                for i in range(BPC):
                    b = n * BPC + i
                    last = pe.matmul(psum[:, self.V_BANK, i * D:(i + 1) * D], xn_t[:, b * P:(b + 1) * P],
                                     self.w_qkv[:, 2, :], start=True, stop=True)
                last.then_inc(self.v_psum, 1)

            def high_parts(self, act, n):
                act.wait_ge(self.xnt_psum, n + 1)
                act.copy(xn_t[:, n * CH:(n + 1) * CH], self.t_bank(n)).then_inc(self.xnt_ready, 1)
                for m in range(2):
                    act.wait_ge(self.proj_done, 2 * n + m + 1)
                    hi = self.parts_of(n, m)[:, 0, :]
                    if self.biased:
                        act.activation(hi, self.qk_bank(n, m), ACT.Identity,
                                       bias=qk_bias[:, m:m + 1]).then_inc(self.hi_ready, 1)
                    else:
                        act.copy(hi, self.qk_bank(n, m)).then_inc(self.hi_ready, 1)

            def low_parts(self, dve, n):
                for m in range(2):
                    dve.wait_ge(self.hi_ready, 2 * n + m + 1)
                    both, src = self.parts_of(n, m), self.qk_bank(n, m)
                    if self.biased:
                        dve.scalar_tensor_tensor(out=both[:, 1, :], in0=src, scalar=qk_bias[:, m:m + 1],
                                                 in1=both[:, 0, :], op0=ALU.add,
                                                 op1=ALU.subtract).then_inc(self.lo_ready, 1)
                    else:
                        dve.tensor_tensor(both[:, 1, :], src, both[:, 0, :], ALU.subtract).then_inc(self.lo_ready, 1)

            def values_out(self, dve, n):
                dve.wait_ge(self.v_psum, n + 1)
                c = self.order[n]
                dst = v_aug[:, c * BPC:(c + 1) * BPC, :, 0:DH]
                src = psum[:, self.V_BANK, :].rearrange("p (b h d) -> p b h d", h=H, d=DH)
                if self.biased:
                    for i in range(BPC):
                        last = dve.tensor_tensor(dst[:, i], src[:, i],
                                                 bv_bc[:, :].rearrange("p (h d) -> p h d", d=DH), ALU.add)
                else:
                    last = dve.tensor_copy(dst, src)
                last.then_inc(self.v_ready, 1)

        def expert_layer(first, order, given, norms, next_norms, released=None, following=None):
            s1, s2 = NormScratch("norm"), NormScratch("norm_out")
            x_parts = parts[:, 0:4 * CH].rearrange("p (n r t) -> p n r t", n=2, r=2)
            logit = sb("logit", [P, BPC, E])
            top = sb("top", [P, BPC])
            tied = sb("tied", [P, BPC, E])
            onehot = sb("onehot", [P, NB, NPART, E], BF16)
            onehot_t = sb("onehot_t", [NPART * E, 2, CH], BF16)
            AHEAD_E, NX = 3, 4
            mask_sb = parts[:, 4 * CH:8 * CH].rearrange("p (k t) -> p k t", k=NX)
            x_mask = parts[:, 8 * CH:16 * CH].rearrange("p (k r t) -> p k r t", k=NX, r=2)
            y = x_plus
            MASK_BANKS, DOWN_BANK, PREP_BANK = 4, 6, 7

            xnt_psum, xhi_ready, xnt_ready = sem("xnt_psum"), sem("xhi_ready"), sem("xnt_ready")
            xlo_ready = sem("xlo_ready")
            logits_done, onehot_ready = sem("logits_done"), sem("onehot_ready")
            oht_psum, oht_ready = sem("oht_psum"), sem("oht_ready")
            mask_psum, mask_ready, xmask_ready = sem("mask_psum"), sem("mask_ready"), sem("xmask_ready")
            expert_mm, experts_done = sem("expert_mm"), sem("experts_done")
            gelu_done, down_done, y_ready = sem("gelu_done"), sem("down_done"), sem("y_ready")
            pool_pre = sem("pool_pre")


            if first:
                x_loaded = [sem(f"x_loaded{n}") for n in range(2)]
                w1_loaded = [sem(f"w1_loaded{n}") for n in range(2)]
                router_loaded, later_loaded = sem("router_loaded"), sem("later_loaded")
                N_LATER = 16
                masks_zeroed, masks_done, slots_set = sem("masks_zeroed"), sem("masks_done"), sem("slots_set")
                wmax_ready, wmax_turned, wmax_one, wmax_all = sem("wmax_ready"), sem("wmax_turned"), sem("wmax_one"), sem("wmax_all")
                wr_turned, wr_ready, w1_split = sem("wr_turned"), sem("wr_ready"), sem("w1_split")
                b1_split_ready, b1_moved = sem("b1_split_ready"), sem("b1_moved")
                sums_ready, total_ready, tern_ready, tern_turned, tern_copied = (
                    sem("sums_ready"), sem("total_ready"), sem("tern_ready"), sem("tern_turned"), sem("tern_copied"))
                w1_in = q_slots[:, :, :].rearrange("p a t -> p (a t)").bitcast(F32).rearrange("p (e i) -> p e i", e=E)

                taken = [0]

                def staged(cols, rows=P):
                    taken[0] += 1
                    return sb(f"staged{taken[0]}", [rows, cols])[:, :]

                aw_in = staged(3 * D).rearrange("p (t d) -> p t d", t=3)
                fw1_in, fw2_in = staged(HT * D), staged(HID)
                below, tern = w1_in[:, 0:2, :], w1_in[:, 2:4, :]
                gam_in, bet_in, fb2_in = staged(D), staged(D), staged(D)
                wr_in, col_in = staged(D, E), staged(D, 2 + HT)
                b1_in, b1_rest = hidden[0:E, 0, 0, :], hidden[0:E, 0, 1, :]
                b1_split = hidden[0:E, 1, 0:2, :].rearrange("p t i -> p (t i)").bitcast(BF16).rearrange(
                    "p (r i) -> p r i", i=HID)
                wmax = sb("wmax", [P, 3])
                wmax_col = sb("wmax_col", [P, 1])
                wmax_row = sb("wmax_row", [1, 1])
                exponent = sb("exponent", [P, 1])
                abs_sum = sb("abs_sum", [P, 2])
                half_gamma = sb("half_gamma", [P, 2, 2])
                qk_max = sb("qk_max", [P, 3])
                qk_max_row = sb("qk_max_row", [3, 1])
                qk_max_diag = sb("qk_max_diag", [3, 3])
                qk_scale = sb("qk_scale", [P, 2])
                qk_exponent = sb("qk_exponent", [P, 2])
                qk_unscale = sb("qk_unscale", [P, 2])
                qk_max_ready, qk_max_turned, qk_diag_ready, qk_max_all = (
                    sem("qk_max_ready"), sem("qk_max_turned"), sem("qk_diag_ready"), sem("qk_max_all"))
                rest_rows_stored, qk_scaled = sem("rest_rows_stored"), sem("qk_scaled")


            if first:
                def row(ap):
                    return bass.AP(tensor=ap.tensor, offset=ap.offset, ap=[[0, P], [1, ap.shape[0]]])

                @blk.sync
                def _(sp):
                    w1_dram = w1.rearrange("e d i -> d e i")
                    sp.dma_start(x_res[:, 0:BPC, :], x_dram[:, 0:BPC, :]).then_inc(x_loaded[0], 16)
                    sp.dma_start(w1_in[:, 0:E // 2, :], w1_dram[:, 0:E // 2, :]).then_inc(w1_loaded[0], 16)
                    sp.dma_start(wr_in, wr).then_inc(router_loaded, 16)
                    sp.dma_start(b1_in, b1).then_inc(router_loaded, 16)
                    sp.dma_start(w1_in[:, E // 2:E, :], w1_dram[:, E // 2:E, :]).then_inc(w1_loaded[1], 16)
                    sp.dma_start(x_res[:, BPC:NB, :], x_dram[:, BPC:NB, :]).then_inc(x_loaded[1], 16)
                    for dst, src in ((bo2_bc[:, :], row(bo2)),
                                     (wo2_sb[:, :, :], wo2.rearrange("(t p) d -> p t d", p=P)),
                                     (gam_in, row(gamma)), (bet_in, row(beta)), (fb2_in, row(fb2)),
                                     (fw1_in.rearrange("p (t d) -> p t d", t=HT), fw1.rearrange("(t p) d -> p t d", p=P)),
                                     (fw2_in, fw2), (aw_in, aw.rearrange("(t p) d -> p t d", p=P)),
                                     (col_in[0:2, :], ab[0:2 * D].rearrange("(t p) -> t p", p=P)),
                                     (col_in[2:2 + HT, :], fb1.rearrange("(t p) -> t p", p=P)),
                                     (w_qkv0[:, 0, :], wq), (w_qkv0[:, 1, :], wk), (w_qkv0[:, 2, :], wv),
                                     (wo_sb[:, :], wo), (bo_bc[:, :], row(bo)), (bv_bc[:, :], row(ab[2 * D:3 * D]))):
                        sp.dma_start(dst, src).then_inc(later_loaded, 16)
                    sp.wait_ge(b1_split_ready, 1)
                    for r in range(NPART):
                        sp.dma_start(b1_parts[r * E:(r + 1) * E, :], b1_split[:, r, :]).then_inc(b1_moved, 16)
                    sp.wait_ge(slots_set, 2)
                    sp.dma_start(slot_dram[0][:, TERMS, :, :],
                                 k_slots[:, 1, :]).then_inc(rest_rows_stored, 16)
                    sp.dma_start(slot_dram[1][:, TERMS, MAX_PARTS:DH, :],
                                 k_slots[0:H * (DH - MAX_PARTS), 1, :]).then_inc(rest_rows_stored, 16)
                    sp.dma_start(slot_dram[1][:, TERMS, 0:MAX_PARTS, :],
                                 k_slots[0:H * MAX_PARTS, 0, :]).then_inc(rest_rows_stored, 16)
                    sp.wait_ge(rest_rows_stored, 16 * 3)
                    sp.wait_ge(b1_moved, 16 * NPART)
                    sp.wait_ge(later_loaded, 16 * N_LATER)

            @blk.tensor
            def _(pe):
                def transposes(n):
                    norms.wait(pe, order[n])
                    if n >= 1:
                        pe.wait_ge(oht_ready, n)
                    for i in range(BPC):
                        last = pe.transpose(psum[:, PREP_BANK, i * P:(i + 1) * P], xn[:, order[n] * BPC + i, :], ident[:, :])
                    last.then_inc(xnt_psum, 1)

                def logits(n):
                    pe.wait_ge(xnt_ready, n + 1)
                    if first and n == 0:
                        pe.wait_ge(wr_ready, 1)
                    for i in range(BPC):
                        last = pe.matmul(psum[:, PREP_BANK, i * E:(i + 1) * E], xn_t[:, n * CH + i * P:n * CH + (i + 1) * P],
                                         wr_t[:, :], start=True, stop=True)
                    last.then_inc(logits_done, 1)

                def choices(n):
                    pe.wait_ge(onehot_ready, n + 1)
                    bank = psum[0:NPART * E, PREP_BANK, 0:CH // 2].bitcast(BF16)
                    for i in range(BPC):
                        last = pe.transpose(bank[:, i * P:(i + 1) * P],
                                            onehot[:, n * BPC + i, :, :].rearrange("p r e -> p (r e)"), ident_bf[:, :])
                    last.then_inc(oht_psum, 1)

                def masks_of(k):
                    n, e = divmod(k, E)
                    if k >= 2:
                        pe.wait_ge(mask_ready, k - 1)
                    pe.wait_ge(onehot_ready, n + 1)
                    for i in range(BPC):
                        last = pe.matmul(psum[:, MASK_BANKS + k % 2, i * P:(i + 1) * P],
                                         onehot[:, n * BPC + i, 0, e:e + 1].broadcast_to([P, P]), ident_bf[:, :],
                                         start=True, stop=True)
                    last.then_inc(mask_psum, 1)

                def expert(k):
                    n, e = divmod(k, E)
                    pe.wait_ge(xmask_ready, k + 1)
                    if first and n == 0:
                        pe.wait_ge(w1_split, e + 1)
                    for t in range(HT):
                        if e == 0 and n >= 1:
                            pe.wait_ge(gelu_done, HT * (n - 1) + t + 1)
                        for wp, xp in ((0, 0), (0, 1), (1, 0)):
                            last = pe.matmul(psum[:, t, :], w1_parts[:, e, wp, t * P:(t + 1) * P],
                                             x_mask[:, k % NX, xp, :], start=(e == 0 and (wp, xp) == (0, 0)),
                                             stop=False)
                    last.then_inc(expert_mm, 1)

                def biases(n):
                    pe.wait_ge(oht_ready, n + 1)
                    if first and n == 0:
                        pe.wait_ge(b1_moved, 16 * NPART)
                    for t in range(HT):
                        pe.matmul(psum[:, t, :], b1_parts[:, t * P:(t + 1) * P], onehot_t[:, n % 2, :],
                                  start=False, stop=True).then_inc(experts_done, 1)

                def down(n):
                    pe.wait_ge(gelu_done, HT * (n + 1))
                    if n >= 1:
                        pe.wait_ge(y_ready, n)
                    if first and n == 0:
                        pe.wait_ge(later_loaded, 16 * N_LATER)
                    if first and n == 2:
                        pe.wait_ge(tern_copied, 1)
                    for i in range(BPC):
                        for t in range(HT):
                            last = pe.matmul(psum[:, DOWN_BANK, i * D:(i + 1) * D],
                                             hidden[:, n % 2, t, i * P:(i + 1) * P], wo2_sb[:, t, :],
                                             start=(t == 0), stop=(t == HT - 1))
                    last.then_inc(down_done, 1)

                def weights_max():
                    pe.wait_ge(masks_done, 6)
                    pe.wait_ge(router_loaded, 32)
                    pe.transpose(psum[:, 1, 0:E], wr_in, ident[0:E, 0:E]).then_inc(wr_turned, 1)
                    transposes(0)
                    pe.wait_ge(wmax_ready, 1)
                    pe.transpose(psum[0:1, 0, 0:P], wmax_col[:, :], ident[:, :]).then_inc(wmax_turned, 1)
                    logits(0)
                    pe.wait_ge(wmax_one, 1)
                    pe.matmul(psum[:, 0, P:P + 1], ones_mat[0:1, :], wmax_row[:, :], start=True,
                              stop=True).then_inc(wmax_all, 1)

                def other_weights_a():
                    pe.wait_ge(oht_ready, 3)
                    pe.wait_ge(sums_ready, 2)
                    pe.matmul(psum[:, PREP_BANK, 0:2], ones_mat[:, :], abs_sum[:, :], start=True, stop=True)
                    pe.transpose(psum[:, PREP_BANK, 2:4 + HT], col_in, ident[0:2 + HT, 0:2 + HT])
                    for t in range(3):
                        last = pe.transpose(psum[:, PREP_BANK, (t + 1) * P:(t + 2) * P], aw_in[:, t, :], ident[:, :])
                    last.then_inc(total_ready, 1)

                def qk_scales(part):
                    if part == 0:
                        pe.wait_ge(tern_copied, 1)
                        pe.wait_ge(qk_max_ready, 1)
                        pe.transpose(psum[0:3, PREP_BANK, 0:P], qk_max[:, :], ident[:, :]).then_inc(qk_max_turned, 1)
                    else:
                        pe.wait_ge(qk_diag_ready, 1)
                        pe.matmul(psum[:, PREP_BANK, P:P + 3], ones_mat[0:3, :], qk_max_diag[:, :], start=True,
                                  stop=True).then_inc(qk_max_all, 1)

                def other_weights_b():
                    pe.wait_ge(tern_ready, 2)
                    pe.wait_ge(y_ready, 2)
                    pe.wait_ge(oht_ready, NCH)
                    for bank, m in ((PREP_BANK, 0), (DOWN_BANK, 1)):
                        for t in range(HT):
                            last = pe.transpose(psum[:, bank, t * P:(t + 1) * P], tern[:, m, t * P:(t + 1) * P],
                                                ident[:, :])
                    last.then_inc(tern_turned, 1)

                if released:
                    pe.wait_ge(*released)
                if first:
                    weights_max()
                else:
                    transposes(0)
                    logits(0)
                choices(0)
                for k in range(AHEAD_E):
                    masks_of(k)
                for n in range(NCH):
                    for e in range(E):
                        k = n * E + e
                        if k + AHEAD_E < NCH * E:
                            masks_of(k + AHEAD_E)
                        expert(k)
                        if e == 0 and n + 1 < NCH:
                            transposes(n + 1)
                        if e == 1 and n + 1 < NCH:
                            logits(n + 1)
                        if e == 2 and n >= 1:
                            down(n - 1)
                        if e == 3 and n + 1 < NCH:
                            choices(n + 1)
                        if first and (n, e) == (1, 5):
                            other_weights_a()
                        if first and (n, e) == (2, 6):
                            other_weights_b()
                        if first and (n, e) in ((3, 0), (3, 2)):
                            qk_scales(e // 2)
                        if following and (n, e) == (3, 5):
                            pe.wait_ge(mask_ready, NCH * E)
                            following.transposes(pe, 0)
                        if following and (n, e) == (3, 6):
                            if first:
                                pe.wait_ge(qk_scaled, 1)
                            following.queries_keys(pe, 0)
                    biases(n)
                down(NCH - 1)

            @blk.scalar
            def _(act):
                def transposed(n):
                    act.wait_ge(xnt_psum, n + 1)
                    if n >= 2:
                        act.wait_ge(xmask_ready, E * (n - 1))
                        act.wait_ge(logits_done, n - 1)
                    act.activation(x_parts[:, n % 2, 0, :], psum[:, PREP_BANK, :], ACT.Copy,
                                   scale=X_SCALE).then_inc(xhi_ready, 1)
                    act.copy(xn_t[:, n * CH:(n + 1) * CH], psum[:, PREP_BANK, :]).then_inc(xnt_ready, 1)

                def choices(n):
                    act.wait_ge(oht_psum, n + 1)
                    if n >= 2:
                        act.wait_ge(experts_done, HT * (n - 1))
                    act.copy(onehot_t[:, n % 2, :],
                             psum[0:NPART * E, PREP_BANK, 0:CH // 2].bitcast(BF16)).then_inc(oht_ready, 1)

                def gelus(n):
                    for t in range(HT):
                        act.wait_ge(experts_done, n * HT + t + 1)
                        if n >= 2:
                            act.wait_ge(down_done, n - 1)
                        act.activation(hidden[:, n % 2, t, :], psum[:, t, :], ACT.Gelu,
                                       scale=unscale[:, 0:1]).then_inc(gelu_done, 1)

                transposed(0)
                choices(0)
                for k in range(NCH * E):
                    act.wait_ge(mask_psum, k + 1)
                    if k >= NX:
                        act.wait_ge(xmask_ready, k - NX + 1)
                    act.copy(mask_sb[:, k % NX, :], psum[:, MASK_BANKS + k % 2, :]).then_inc(mask_ready, 1)
                    n, e = divmod(k, E)
                    if e == AHEAD_E and n + 1 < NCH:
                        transposed(n + 1)
                    if e == 3 + AHEAD_E and n + 1 < NCH:
                        choices(n + 1)
                    if e == AHEAD_E - 1 and n >= 1:
                        gelus(n - 1)
                if following:
                    following.high_parts(act, 0)
                gelus(NCH - 1)

            @blk.gpsimd
            def _(pool):
                if first:
                    pool.memset(ident[:, :], 0.0).then_inc(masks_zeroed, 1)
                    pool.memset(ident_bf[:, :], 0.0).then_inc(masks_zeroed, 1)
                    pool.memset(causal_add[:, :], 0.0).then_inc(masks_zeroed, 1)
                    pool.memset(later_keys[:, :], 0.0).then_inc(masks_zeroed, 1)
                    pool.memset(ones_mat[:, :], 1.0).then_inc(masks_done, 1)
                    pool.wait_ge(masks_zeroed, 4)
                    pool.affine_select(out=ident[:, :], in_=ident[:, :], compare_op=ALU.not_equal, fill=1.0,
                                       base=0, pattern=[[-1, P]], channel_multiplier=1).then_inc(masks_done, 1)
                    pool.affine_select(out=ident_bf[:, :], in_=ident_bf[:, :], compare_op=ALU.not_equal, fill=1.0,
                                       base=0, pattern=[[-1, P]], channel_multiplier=1).then_inc(masks_done, 1)
                    pool.affine_select(out=causal_add[:, CH - P:CH], in_=causal_add[:, CH - P:CH],
                                       compare_op=ALU.is_ge, fill=NEG, base=0, pattern=[[-1, P]],
                                       channel_multiplier=1).then_inc(masks_done, 1)
                    pool.affine_select(out=later_keys[:, :], in_=later_keys[:, :], compare_op=ALU.is_ge, fill=NEG,
                                       base=0, pattern=[[1, P]], channel_multiplier=-1).then_inc(masks_done, 1)
                    pool.iota(rank[:, :], pattern=[[-1, E]], base=E, channel_multiplier=0,
                              allow_small_or_imprecise_dtypes=True).then_inc(masks_done, 1)
                    pool.memset(k_slots[:, :, :].rearrange("p h t -> p (h t)").bitcast(I32), 0).then_inc(slots_set, 1)
                    pool.wait_ge(slots_set, 1)
                    pool.memset(k_slots[0:H * MAX_PARTS, 0, :], MAX_UNIT).then_inc(slots_set, 1)
                    pool.wait_ge(later_loaded, 16 * N_LATER)
                    pool.wait_ge(sums_ready, 2)
                for n in range(NCH):
                    lo, hi = order[n] * BPC, (order[n] + 1) * BPC
                    norms.wait(pool, order[n])
                    pool.tensor_tensor(x_plus[:, lo:hi, :], xn[:, lo:hi, :], bcast_blocks(bo2_bc, BPC),
                                       ALU.add).then_inc(pool_pre, 1)
                    pool.tensor_tensor(x_res[:, lo:hi, :], x_res[:, lo:hi, :], bcast_blocks(beta_half, BPC),
                                       ALU.add).then_inc(pool_pre, 1)

            @blk.vector
            def _(dve):
                own = dve_chain.on(dve)

                def normalise(n):
                    norms.make(dve, own, s1, order[n])

                def rest_of_x(n):
                    dve.wait_ge(xhi_ready, n + 1)
                    dve.wait_ge(xnt_ready, n + 1)
                    dve.scalar_tensor_tensor(out=x_parts[:, n % 2, 1, :], in0=xn_t[:, n * CH:(n + 1) * CH], scalar=X_SCALE,
                                             in1=x_parts[:, n % 2, 0, :], op0=ALU.mult,
                                             op1=ALU.subtract).then_inc(xlo_ready, 1)

                def choose(n):
                    def per_block(ap):
                        return ap.rearrange("p (b a) -> p b a", a=1).broadcast_to([P, BPC, E])

                    dve.wait_ge(logits_done, n + 1)
                    own(dve.tensor_copy(logit[:, :, :], psum[:, PREP_BANK, 0:BPC * E].rearrange("p (b e) -> p b e", e=E)))
                    own.wait()
                    own(dve.tensor_reduce(top[:, :], logit[:, :, :], axis=AX.X, op=ALU.max))
                    own.wait()
                    own(dve.tensor_tensor(tied[:, :, :], logit[:, :, :], per_block(top[:, :]), ALU.is_ge))
                    own.wait()
                    if first and n == 0:
                        dve.wait_ge(masks_done, 6)
                    rank_b = rank[:, :].rearrange("p (a e) -> p a e", a=1).broadcast_to([P, BPC, E])
                    own(dve.tensor_tensor(tied[:, :, :], tied[:, :, :], rank_b, ALU.mult))
                    own.wait()
                    own(dve.tensor_reduce(top[:, :], tied[:, :, :], axis=AX.X, op=ALU.max))
                    own.wait()
                    for r in range(NPART):
                        last = own(dve.tensor_tensor(onehot[:, n * BPC:(n + 1) * BPC, r, :], tied[:, :, :],
                                                     per_block(top[:, :]), ALU.is_equal)) if r < NPART - 1 else \
                            dve.tensor_tensor(onehot[:, n * BPC:(n + 1) * BPC, r, :], tied[:, :, :],
                                              per_block(top[:, :]), ALU.is_equal)
                    last.then_inc(onehot_ready, 1)

                def finish(n):
                    lo, hi = order[n] * BPC, (order[n] + 1) * BPC
                    dve.wait_ge(down_done, n + 1)
                    dve.wait_ge(pool_pre, 2 * (n + 1))
                    dve.tensor_tensor(y[:, lo:hi, :], psum[:, DOWN_BANK, :].rearrange("p (b d) -> p b d", d=D),
                                      x_plus[:, lo:hi, :], ALU.add).then_inc(y_ready, 1)
                    dve.wait_ge(y_ready, n + 1)
                    norm_stats(dve, own, s2, y, lo, BPC)
                    norm_rstd(dve, own, s2, 1e-12, lo, BPC)
                    for b in range(lo, hi):
                        own(norm_apply(dve, s2, xn, y, b))
                    own.wait()
                    own(dve.tensor_tensor(y[:, lo:hi, :], xn[:, lo:hi, :], bcast_blocks(gamma_half, BPC), ALU.mult))
                    own.wait()
                    own(dve.tensor_tensor(x_res[:, lo:hi, :], y[:, lo:hi, :], x_res[:, lo:hi, :], ALU.add))

                def next_norm(n):
                    next_norms.make(dve, own, s1, order[n])

                def scale_of_w1():
                    own(dve.memset(wmax[:, :], 0.0))
                    own.wait()
                    for half in range(2):
                        dve.wait_ge(w1_loaded[half], 16)
                        own(dve.tensor_reduce(wmax[:, half:half + 1], w1_in[:, half * E // 2:(half + 1) * E // 2, :],
                                              axis=AX.XY, op=ALU.max, apply_absolute_value=True))
                    dve.wait_ge(router_loaded, 32)
                    own(dve.tensor_reduce(wmax[0:E, 2:3], b1_in, axis=AX.X, op=ALU.max, apply_absolute_value=True))
                    own.wait()
                    dve.tensor_reduce(wmax_col[:, :], wmax[:, :], axis=AX.X, op=ALU.max).then_inc(wmax_ready, 1)
                    dve.wait_ge(wr_turned, 1)
                    dve.tensor_copy(wr_t[:, :], psum[:, 1, 0:E]).then_inc(wr_ready, 1)
                    dve.wait_ge(wmax_turned, 1)
                    dve.tensor_reduce(wmax_row[:, :], psum[0:1, 0, 0:P], axis=AX.X, op=ALU.max).then_inc(wmax_one, 1)
                    rest_of_x(0)
                    choose(0)
                    dve.wait_ge(wmax_all, 1)
                    own(dve.tensor_scalar(wmax_col[:, :], psum[:, 0, P:P + 1], 2.0 ** -100, None, ALU.max))
                    own.wait()
                    own(dve.tensor_scalar(exponent[:, :].bitcast(I32), wmax_col[:, :].bitcast(I32), 23, None,
                                          ALU.arith_shift_right))
                    own.wait()
                    own(dve.tensor_scalar(w1_scale[:, :].bitcast(I32), exponent[:, :].bitcast(I32),
                                          -float(2 ** 23), float((127 + 127 + 14) * 2 ** 23), ALU.mult, ALU.add))
                    own(dve.tensor_scalar(unscale[:, :].bitcast(I32), exponent[:, :].bitcast(I32),
                                          float(2 ** 23), float(-(14 + 12) * 2 ** 23), ALU.mult, ALU.add))
                    own.wait()

                def split_w1(e):
                    own(dve.tensor_scalar(w1_parts[:, e, 0, :], w1_in[:, e, :], w1_scale[:, 0:1], None, ALU.mult))
                    own.wait()
                    dve.scalar_tensor_tensor(out=w1_parts[:, e, 1, :], in0=w1_in[:, e, :], scalar=w1_scale[:, 0:1],
                                             in1=w1_parts[:, e, 0, :], op0=ALU.mult,
                                             op1=ALU.subtract).then_inc(w1_split, 1)

                def split_b1():
                    own(dve.tensor_scalar(b1_in, b1_in, w1_scale[0:E, 0:1], X_SCALE, ALU.mult, ALU.mult))
                    own.wait()
                    own(dve.tensor_copy(b1_split[:, 0, :], b1_in))
                    own.wait()
                    own(dve.tensor_tensor(b1_rest, b1_in, b1_split[:, 0, :], ALU.subtract))
                    own.wait()
                    own(dve.tensor_copy(b1_split[:, 1, :], b1_rest))
                    own.wait()
                    dve.tensor_tensor(b1_split[:, 2, :], b1_rest, b1_split[:, 1, :],
                                      ALU.subtract).then_inc(b1_split_ready, 1)

                def other_weights_a():
                    own(dve.memset(v_aug[:, :, :, DH:DH + 1], 1.0))
                    dve.wait_ge(later_loaded, 16 * N_LATER)
                    own(dve.tensor_scalar(gamma_half[:, :], gam_in, 0.5, None, ALU.mult))
                    own(dve.tensor_scalar(beta_half[:, :], bet_in, 0.5, None, ALU.mult))
                    own(dve.tensor_scalar(fb2_half[:, :], fb2_in, 0.5, None, ALU.mult))
                    for m, src in ((0, fw1_in), (1, fw2_in)):
                        dve.tensor_reduce(abs_sum[:, m:m + 1], src, axis=AX.X, op=ALU.add,
                                          apply_absolute_value=True).then_inc(sums_ready, 1)

                def other_weights_b():
                    dve.wait_ge(total_ready, 1)
                    for s, sign in ((0, 0.5), (1, -0.5)):
                        own(dve.tensor_scalar(half_gamma[:, s, :], psum[:, PREP_BANK, 0:2], 1.0 / (HID * D), 1e-5,
                                              ALU.mult, ALU.add))
                        own.wait()
                        own(dve.tensor_scalar(half_gamma[:, s, :], half_gamma[:, s, :], sign, None, ALU.mult))
                    own.wait()
                    for m, src in ((0, fw1_in), (1, fw2_in)):
                        own(dve.tensor_scalar(below[:, m, :], src, half_gamma[:, 1, m:m + 1], None, ALU.is_lt))
                        own.wait()
                        dve.scalar_tensor_tensor(out=tern[:, m, :], in0=src, scalar=half_gamma[:, 0, m:m + 1],
                                                 in1=below[:, m, :], op0=ALU.is_gt,
                                                 op1=ALU.subtract).then_inc(tern_ready, 1)
                    own(dve.tensor_copy(bias_cols[:, :], psum[:, PREP_BANK, 2:4 + HT]))
                    own(dve.tensor_copy(w_qkv1[:, :, :], psum[:, PREP_BANK, P:4 * P].rearrange("p (t d) -> p t d", t=3)))
                    own.wait()

                def other_weights_c():
                    dve.wait_ge(tern_turned, 1)
                    own(dve.tensor_copy(tw1_t[:, :, :], psum[:, PREP_BANK, :].rearrange("p (t f) -> p t f", t=HT)))
                    dve.tensor_copy(tw2_t[:, :, :],
                                    psum[:, DOWN_BANK, :].rearrange("p (t d) -> p t d", t=HT)).then_inc(tern_copied, 1)

                def qk_scales(part):
                    if part == 0:
                        own(dve.memset(qk_max[:, :], 0.0))
                        own.wait()
                        own(dve.tensor_reduce(qk_max[:, 0:1], w_qkv0[:, 0:2, :], axis=AX.XY, op=ALU.max,
                                              apply_absolute_value=True))
                        own(dve.tensor_reduce(qk_max[:, 1:2], w_qkv1[:, 0:2, :], axis=AX.XY, op=ALU.max,
                                              apply_absolute_value=True))
                        dve.tensor_reduce(qk_max[:, 2:3], bias_cols[:, 0:2], axis=AX.X, op=ALU.max,
                                          apply_absolute_value=True).then_inc(qk_max_ready, 1)
                    elif part == 1:
                        dve.wait_ge(qk_max_turned, 1)
                        own(dve.tensor_reduce(qk_max_row[:, :], psum[0:3, PREP_BANK, 0:P], axis=AX.X, op=ALU.max))
                        own.wait()
                        dve.tensor_scalar(qk_max_diag[:, :], ident[0:3, 0:3], qk_max_row[:, 0:1], None,
                                          ALU.mult).then_inc(qk_diag_ready, 1)
                    else:
                        dve.wait_ge(qk_max_all, 1)
                        own(dve.tensor_scalar(qk_scale[:, :], psum[:, PREP_BANK, P:P + 2], float(D), 2.0 ** -30,
                                              ALU.mult, ALU.max))
                        own.wait()
                        own(dve.tensor_tensor(qk_scale[:, 1:2], qk_scale[:, 1:2], psum[:, PREP_BANK, P + 2:P + 3],
                                              ALU.max))
                        own.wait()
                        own(dve.tensor_scalar(qk_exponent[:, :].bitcast(I32), qk_scale[:, :].bitcast(I32), 23, None,
                                              ALU.arith_shift_right))
                        own.wait()
                        own(dve.tensor_scalar(qk_scale[:, :].bitcast(I32), qk_exponent[:, :].bitcast(I32),
                                              -float(2 ** 23), float((127 + 127 + 11) * 2 ** 23), ALU.mult, ALU.add))
                        own(dve.tensor_scalar(qk_unscale[:, :].bitcast(I32), qk_exponent[:, :].bitcast(I32),
                                              float(2 ** 23), float(-11 * 2 ** 23), ALU.mult, ALU.add))
                        own.wait()
                        own(dve.scalar_tensor_tensor(out=exp_scale[:, :], in0=qk_unscale[:, :], scalar=SCALE,
                                                     in1=qk_unscale[:, :], op0=ALU.mult, op1=ALU.mult))
                        for layer, w in ((0, w_qkv0), (1, w_qkv1)):
                            own(dve.tensor_scalar(w[:, 0:2, :], w[:, 0:2, :], qk_scale[:, layer:layer + 1], None,
                                                  ALU.mult))
                        dve.tensor_scalar(bias_cols[:, 0:2], bias_cols[:, 0:2], qk_scale[:, 1:2], None,
                                          ALU.mult).then_inc(qk_scaled, 1)

                if first:
                    dve.wait_ge(x_loaded[0], 16)
                if given < 1:
                    normalise(0)
                if first:
                    scale_of_w1()
                else:
                    rest_of_x(0)
                    choose(0)
                for k in range(NCH * E):
                    n, e = divmod(k, E)
                    if first and n == 0:
                        split_w1(e)
                    dve.wait_ge(mask_ready, k + 1)
                    dve.wait_ge(xlo_ready, n + 1)
                    if k >= NX:
                        dve.wait_ge(expert_mm, k - NX + 1)
                    dve.tensor_tensor(x_mask[:, k % NX, :, :], x_parts[:, n % 2, :, :],
                                      mask_sb[:, k % NX, :].rearrange("p (a t) -> p a t", a=1).broadcast_to([P, 2, CH]),
                                      ALU.mult).then_inc(xmask_ready, 1)
                    if e == 1 and given <= n + 1 < NCH:
                        if first and n == 0:
                            dve.wait_ge(x_loaded[1], 16)
                        normalise(n + 1)
                    if e == 3 and n + 1 < NCH:
                        rest_of_x(n + 1)
                    if e == 4 and n + 1 < NCH:
                        choose(n + 1)
                    if e == 5 and n >= 1:
                        finish(n - 1)
                    if following and (n, e) == (3, 7):
                        following.low_parts(dve, 0)
                    if e == 7 and n >= 1:
                        next_norm(n - 1)
                    if first and (n, e) == (0, 3):
                        split_b1()
                    if first and (n, e) == (0, 7):
                        other_weights_a()
                    if first and (n, e) == (1, 7):
                        other_weights_b()
                    if first and (n, e) == (2, 7):
                        other_weights_c()
                        qk_scales(0)
                    if first and n == 3 and e in (2, 4):
                        qk_scales(e // 2)
                finish(NCH - 1)

            return y_ready, NCH


        def ternary_layer(last_layer, order, given, norms, next_norms, released, following=None):
            s1 = NormScratch("norm")
            xnt_psum, hi_ready, lo_ready = sem("xnt_psum"), sem("hi_ready"), sem("lo_ready")
            x_parts = parts[:, 0:4 * CH].rearrange("p (n r t) -> p n r t", n=2, r=2)
            up_done, relu_done, down_done = sem("up_done"), sem("relu_done"), sem("down_done")
            pool_pre, x_ready, stored = sem("pool_pre"), sem("x_ready"), sem("stored")



            @blk.tensor
            def _(pe):
                def features(n):
                    norms.wait(pe, order[n])
                    if n >= 2:
                        pe.wait_ge(lo_ready, n - 1)
                    for i in range(BPC):
                        last = pe.transpose(psum[:, 4 + n % 2, i * P:(i + 1) * P], xn[:, order[n] * BPC + i, :], ident[:, :])
                    last.then_inc(xnt_psum, 1)

                def down(n):
                    if n >= 2:
                        pe.wait_ge(x_ready, n - 1)
                    pe.wait_ge(relu_done, HT * (n + 1))
                    for i in range(BPC):
                        for t in range(HT):
                            last = pe.matmul(psum[:, 6 + n % 2, i * D:(i + 1) * D],
                                             hidden[:, n % 2, t, i * P:(i + 1) * P], tw2_t[:, t, :],
                                             start=(t == 0), stop=(t == HT - 1))
                    last.then_inc(down_done, 1)

                if released:
                    pe.wait_ge(*released)
                features(0)
                for n in range(NCH):
                    pe.wait_ge(lo_ready, n + 1)
                    for t in range(HT):
                        if n >= 1:
                            pe.wait_ge(relu_done, HT * (n - 1) + t + 1)
                        for xp in range(2):
                            last = pe.matmul(psum[:, t, :], tw1_t[:, t, :], x_parts[:, n % 2, xp, :],
                                             start=(xp == 0), stop=(xp == 1))
                        last.then_inc(up_done, 1)
                    if n + 1 < NCH:
                        features(n + 1)
                    elif following:
                        following.transposes(pe, 0)
                    if n >= 1:
                        down(n - 1)
                if following:
                    following.queries_keys(pe, 0)
                down(NCH - 1)

            @blk.scalar
            def _(act):
                def features(n):
                    act.wait_ge(xnt_psum, n + 1)
                    if n >= 2:
                        act.wait_ge(up_done, HT * (n - 1))
                    act.activation(x_parts[:, n % 2, 0, :], psum[:, 4 + n % 2, :], ACT.Copy,
                                   scale=X_SCALE).then_inc(hi_ready, 1)

                features(0)
                for n in range(NCH):
                    for t in range(HT):
                        act.wait_ge(up_done, n * HT + t + 1)
                        if n >= 2:
                            act.wait_ge(down_done, n - 1)
                        act.activation(hidden[:, n % 2, t, :], psum[:, t, :], ACT.Relu,
                                       bias=fb1_col[:, t:t + 1], scale=1.0 / X_SCALE).then_inc(relu_done, 1)
                    if n + 1 < NCH:
                        features(n + 1)
                    elif following:
                        following.high_parts(act, 0)

            @blk.gpsimd
            def _(pool):
                for n in range(NCH):
                    lo, hi = order[n] * BPC, (order[n] + 1) * BPC
                    norms.wait(pool, order[n])
                    pool.tensor_tensor(x_plus[:, lo:hi, :], x_res[:, lo:hi, :], bcast_blocks(fb2_half, BPC),
                                       ALU.add).then_inc(pool_pre, 1)

            @blk.vector
            def _(dve):
                own = dve_chain.on(dve)

                def low_part(n):
                    dve.wait_ge(hi_ready, n + 1)
                    dve.scalar_tensor_tensor(out=x_parts[:, n % 2, 1, :], in0=psum[:, 4 + n % 2, :], scalar=X_SCALE,
                                             in1=x_parts[:, n % 2, 0, :], op0=ALU.mult,
                                             op1=ALU.subtract).then_inc(lo_ready, 1)

                late = list(norms.order[given:])
                for n in range(NCH - 1):
                    low_part(n)
                    if late:
                        norms.make(dve, own, s1, late.pop(0))
                dve.wait_ge(norms.ready, NB)
                dve.wait_ge(pool_pre, NCH)
                for n in range(NCH):
                    lo, hi = order[n] * BPC, (order[n] + 1) * BPC
                    if n == 1:
                        low_part(NCH - 1)
                    if following and n == NCH - 1:
                        following.low_parts(dve, 0)
                    dve.wait_ge(down_done, n + 1)
                    dve.scalar_tensor_tensor(out=x_res[:, lo:hi, :].rearrange("p b d -> p (b d)"),
                                             in0=psum[:, 6 + n % 2, :], scalar=0.5,
                                             in1=x_plus[:, lo:hi, :].rearrange("p b d -> p (b d)"),
                                             op0=ALU.mult, op1=ALU.add).then_inc(x_ready, 1)
                    dve.wait_ge(x_ready, n + 1)
                    if not last_layer and n < NCH - 1:
                        next_norms.make(dve, own, s1, order[n])

            @blk.sync
            def _(sp):
                if last_layer:
                    for n in range(NCH):
                        lo, hi = order[n] * BPC, (order[n] + 1) * BPC
                        sp.wait_ge(x_ready, n + 1)
                        sp.dma_start(out_dram[:, lo:hi, :], x_res[:, lo:hi, :]).then_inc(stored, 16)
                    sp.wait_ge(stored, 16 * NCH)

            return x_ready, NCH


        HALF = NG // 2
        STEPS = [(g, c) for c in range(NCH) for g in range(HALF)] + \
                [(g, c) for c in reversed(range(NCH)) for g in range(HALF, NG)]
        AHEAD = 2
        SLACK = 3
        UNIT_FIXED, QUAD_FIXED = 64, 64

        def quads_of(step):
            return [(step, j) for j in range(BPC * (step[1] + 1))]

        def max_units_of(step):
            return [(step, i, kc, h) for i in range(BPC) for kc in range(step[1] + 1) for h in range(G)]

        def columns_of_quad(q):
            (_, c), j = q
            return CH - max(0, j - BPC * c) * P

        def columns_of_unit(u):
            (_, c), i, kc, _ = u
            return CH if kc < c else (i + 1) * P

        def units_beside_quads():
            deadlines, quad_cost, unit_cost = [], [0], [0]
            for n, s in enumerate(STEPS):
                if n >= AHEAD:
                    for u in max_units_of(s):
                        unit_cost.append(unit_cost[-1] + UNIT_FIXED + columns_of_unit(u))
                    deadlines.append((len(quad_cost) - 1 - SLACK, len(unit_cost) - 1))
                for q in quads_of(s):
                    quad_cost.append(quad_cost[-1] + QUAD_FIXED + columns_of_quad(q))
            counts, done = [], 0
            for t in range(len(quad_cost) - 1):
                pace = max([(unit_cost[u] - unit_cost[done]) / (quad_cost[q] - quad_cost[t]) for q, u in deadlines
                            if q > t], default=0)
                target = unit_cost[done] + pace * (quad_cost[t + 1] - quad_cost[t])
                count = 0
                while done + count + 1 < len(unit_cost) and unit_cost[done + count] < target - 1e-6:
                    count += 1
                counts.append(count)
                done += count
            return counts

        TURNS = [t for s in STEPS[:AHEAD] for t in ((None, max_units_of(s)), (None, []))]
        units_left = [u for s in STEPS[AHEAD:] for u in max_units_of(s)]
        for q, count in zip([q for s in STEPS for q in quads_of(s)], units_beside_quads()):
            TURNS.append((q, units_left[:count]))
            units_left = units_left[count:]
        assert not units_left
        TURNS += [(None, [])] * 5

        def attention_layer(proj, layer, projected, given, next_norms, next_given, released):
            s1 = NormScratch("norm")
            ctx = xn
            NP = 4
            probs = hidden[:, :, :, :].rearrange("p a (b c) q -> p (a b) c q", c=2)
            out_t = xn_t[:, 0:2 * CH].rearrange("p (a q) -> p a q", a=2)
            ctx_t = parts[:, :].bitcast(F32)
            recip = sb("recip", [P, 2, BPC, G])
            junk = sb("junk", [P, 2, CH], BF16)
            part_max = sb("part_max", [P, 2, G, BPC, NCH])
            neg_max = sb("neg_max", [P, 2, G * BPC])
            nm_parts = sb("nm_parts", [G * BPC, 2, MAX_PARTS, P], F16)

            parts_stored = [sem(f"parts_stored{i}") for i in range(2)]
            q_landed = [sem(f"q_landed{n}") for n in range(NCH)]
            k_landed = [sem(f"k_landed{n}") for n in range(1, NCH)]



            def load_k_rows(engine, n, h):
                cols = slice(n * CH, (n + 1) * CH)
                return engine.dma_start(k_slots[SLOT * h:SLOT * (h + 1), h::G, cols],
                                        slot_dram[1].rearrange("(g h) i d t -> h (i d) g t", h=G)[h, :, :, cols])



            ring_read, ring_full, o_bank_set = sem("ring_read"), sem("ring_full"), sem("o_bank_set")
            negmax_ready = sem("negmax_ready")
            negmax_landed = [sem(f"negmax_landed{i}") for i in range(4)]
            scores_done, exp_done, pv_done = sem("scores_done"), sem("exp_done"), sem("pv_done")
            out_copied = sem("out_copied")
            S_BANKS, O_BANK, RING_BANKS, RING = 0, 4, 5, 3
            LATE_NORM, LAST_PROJECTION = 1, 3

            step_no = {s: i for i, s in enumerate(STEPS)}
            quad_no = {q: i for i, q in enumerate(q for q, _ in TURNS if q)}
            diagonal = {q for q in quad_no if q[1] >= BPC * q[0][1]}

            def first_query(q):
                (_, c), j = q
                return max(0, j - BPC * c) * P

            def late_work():
                plan, ended_m, ended_q = [], [], []
                for q, units in TURNS:
                    m_now = [u[0] for u in units if u == max_units_of(u[0])[-1]]
                    q_now = [q[0]] if q and q[1] == BPC * (q[0][1] + 1) - 1 else []
                    plan.append((m_now, ended_m[-1] if ended_m else [], ended_q[-1] if ended_q else [],
                                 ended_q[-2] if len(ended_q) > 1 else []))
                    ended_m.append(m_now)
                    ended_q.append(q_now)
                return plan

            PLAN = late_work()

            idle = max(turn for turn, (_, turn_max, _, _) in enumerate(PLAN) if turn_max)
            tail, norm_turn = {}, {}
            for turn, (_, _, _, turn_out) in enumerate(PLAN):
                for g, c in turn_out:
                    if g == NG - 1:
                        if projected:
                            tail.setdefault(turn + 1, []).append(("turned", c))
                            tail.setdefault(turn + 2, []).append(("project", c))
                        if c in next_norms.order[:next_given]:
                            norm_turn[idle + 1 + 3 * (NCH - 1 - c)] = c

            RING_ITEMS, ring_no = [], {}
            for (_, units), (_, turn_max, _, turn_out) in zip(TURNS, PLAN):
                RING_ITEMS.append([("scores", u) for u in units] + [("max", s) for s in turn_max] +
                                  [("out", s) for s in turn_out])
                RING_ITEMS[-1] += tail.get(len(RING_ITEMS) - 1, [])
                for item in RING_ITEMS[-1]:
                    ring_no[item] = len(ring_no)
            last_unit = {s: max(n for item, n in ring_no.items() if item[0] == "scores" and item[1][0] == s)
                         for s in STEPS}

            @blk.tensor
            def _(pe):
                def score_tile(q, pr):
                    (g, c), j = q
                    n = quad_no[q]
                    off = first_query(q)
                    if j == 0 and pr == 0:
                        pe.wait_ge(negmax_landed[step_no[q[0]] % 4], 16 * MAX_PARTS * (step_no[q[0]] // 4 + 1))
                    tile = 2 * n + pr
                    if tile >= 2:
                        pe.wait_ge(exp_done, tile - 1)
                    for par in range(2):
                        last = pe.matmul(psum[:, S_BANKS + 2 * (tile % 2) + par, off:CH],
                                         k_slots[:, G * g + 2 * pr + par, j * P:(j + 1) * P],
                                         q_slots[:, g, c * CH + off:(c + 1) * CH],
                                         start=True, stop=q not in diagonal)
                    if q in diagonal:
                        for par in range(2):
                            last = pe.matmul(psum[:, S_BANKS + 2 * (tile % 2) + par, off:off + P],
                                             ident_bf[:, :], later_keys[:, :], start=False, stop=True)
                    last.then_inc(scores_done, 1)

                def values(q):
                    (g, c), j = q
                    n = quad_no[q]
                    off = first_query(q)
                    pe.wait_ge(exp_done, 2 * n + 2)
                    if j == 0:
                        pe.wait_ge(*((out_copied, step_no[q[0]]) if step_no[q[0]] else (o_bank_set, 1)))
                    for h in range(G):
                        last = pe.matmul(psum[VW * h:VW * h + DH + 1, O_BANK, off:CH],
                                         v_aug[:, j, G * g + h, :],
                                         probs[:, (2 * n + h // 2) % NP, h % 2, off:CH],
                                         start=(j == 0), stop=(j == BPC * (c + 1) - 1))
                    last.then_inc(pv_done, 1)

                def ring_item(item):
                    kind, what = item
                    n = ring_no[item]
                    bank = RING_BANKS + n % RING
                    if n >= RING:
                        pe.wait_ge(ring_read, n - RING + 1)
                    if kind == "scores":
                        (g, c), i, kc, h = what
                        if (g, i, kc, h) == (0, 0, 0, 0):
                            pe.wait_ge(q_landed[c], 16 if c else 16 * (G + 1))
                            if c:
                                pe.wait_ge(k_landed[c - 1], 16 * G)
                        w = CH if kc < c else (i + 1) * P
                        qb = BPC * c + i
                        last = pe.matmul(psum[:, bank, 0:w], q_slots[:, g, qb * P:(qb + 1) * P],
                                         k_slots[:, G * g + h, kc * CH:kc * CH + w], start=True, stop=True)
                    elif kind == "max":
                        k = step_no[what]
                        pe.wait_ge(negmax_ready, k + 1)
                        last = pe.transpose(psum[0:G * BPC, bank, 0:P], neg_max[:, k % 2, :], ident[:, :])
                    elif kind == "turned":
                        pe.wait_ge(ring_read, ring_no["out", (NG - 1, what)] + 1)
                        for i in range(BPC):
                            last = pe.transpose(psum[:, bank, i * P:(i + 1) * P], ctx[:, what * BPC + i, :], ident[:, :])
                    elif kind == "project":
                        pe.wait_ge(ring_read, ring_no["turned", what] + 1)
                        for i in range(BPC):
                            b = what * BPC + i
                            last = pe.matmul(psum[:, bank, i * D:(i + 1) * D], ctx_t[:, b * P:(b + 1) * P],
                                             wo_sb[:, :], start=True, stop=True)
                    else:
                        k = step_no[what]
                        pe.wait_ge(out_copied, k + 1)
                        for i in range(BPC):
                            last = pe.transpose(psum[:, bank, i * P:(i + 1) * P],
                                                out_t[:, k % 2, i * P:(i + 1) * P], ident[:, :])
                    last.then_inc(ring_full, 1)

                for n in range(NCH - 1):
                    if n >= 1:
                        proj.queries_keys(pe, n)
                    if n + 1 < NCH - 1:
                        proj.transposes(pe, n + 1)
                    proj.values(pe, n)
                pe.wait_ge(*released)
                previous = None
                for turn, ((q, _), items) in enumerate(zip(TURNS, RING_ITEMS)):
                    if turn == LAST_PROJECTION:
                        proj.transposes(pe, NCH - 1)
                        proj.queries_keys(pe, NCH - 1)
                        proj.values(pe, NCH - 1)
                    if turn == LAST_PROJECTION + 1:
                        pe.wait_ge(proj.lo_ready, 2 * NCH)
                        pe.wait_ge(proj.v_ready, NCH)
                    cuts = [0, len(items) // 4, len(items) // 2 + len(items) // 4, len(items)]
                    if q:
                        score_tile(q, 0)
                    for item in items[cuts[0]:cuts[1]]:
                        ring_item(item)
                    if q:
                        score_tile(q, 1)
                    for item in items[cuts[1]:cuts[2]]:
                        ring_item(item)
                    if previous:
                        values(previous)
                    for item in items[cuts[2]:cuts[3]]:
                        ring_item(item)
                    previous = q

            @blk.scalar
            def _(act):
                for n in range(1, NCH):
                    proj.high_parts(act, n)
                for (q, _), (_, _, copy_out, _) in zip(TURNS, PLAN):
                    if q:
                        n = quad_no[q]
                        off = first_query(q)
                        for pr in range(2):
                            tile = 2 * n + pr
                            act.wait_ge(scores_done, tile + 1)
                            if tile >= NP:
                                act.wait_ge(pv_done, (tile - NP) // 2 + 1)
                            bank = S_BANKS + 2 * (tile % 2)
                            act.activation(probs[:, tile % NP, :, off:CH], psum[:, bank:bank + 2, off:CH],
                                           ACT.Exp, scale=exp_scale[:, layer:layer + 1]).then_inc(exp_done, 1)
                    for s in copy_out:
                        k = step_no[s]
                        last_quad = quad_no[(s, BPC * (s[1] + 1) - 1)]
                        act.wait_ge(pv_done, last_quad + 1)
                        if k >= 2:
                            act.wait_ge(ring_full, ring_no["out", STEPS[k - 2]] + 1)
                        act.copy(out_t[:, k % 2, :], psum[:, O_BANK, :]).then_inc(out_copied, 1)

            @blk.vector
            def _(dve):
                own = dve_chain.on(dve)

                dve.memset(psum[:, O_BANK, :], 0.0).then_inc(o_bank_set, 1)
                for n in range(NCH - 1):
                    if n >= 1:
                        proj.low_parts(dve, n)
                    proj.values_out(dve, n)
                junk_used = [0, 0]
                for turn, (items, (m_now, _, _, _)) in enumerate(zip(RING_ITEMS, PLAN)):
                    if turn == LATE_NORM:
                        for chunk in proj.norms.order[given:]:
                            proj.norms.make(dve, own, s1, chunk)
                    if turn == LAST_PROJECTION:
                        proj.low_parts(dve, NCH - 1)
                        proj.values_out(dve, NCH - 1)
                        dve.wait_ge(proj.xnt_psum, NCH)
                    for item in items:
                        kind, what = item
                        n = ring_no[item]
                        bank = RING_BANKS + n % RING
                        dve.wait_ge(ring_full, n + 1)
                        if kind == "scores":
                            s, i, kc, h = what
                            dst = part_max[:, step_no[s] % 2, h, i, kc:kc + 1]
                            if kc < s[1]:
                                dve.tensor_reduce(dst, psum[:, bank, :], axis=AX.X,
                                                  op=ALU.max).then_inc(ring_read, 1)
                            else:
                                w = (i + 1) * P
                                if junk_used[n % 2]:
                                    dve.wait_ge(ring_read, junk_used[n % 2])
                                dve.tensor_tensor_reduce(out=junk[:, n % 2, 0:w], in0=psum[:, bank, 0:w],
                                                         in1=causal_add[:, CH - w:CH], scale=1.0,
                                                         scalar=-3.0e38, op0=ALU.add, op1=ALU.max,
                                                         accum_out=dst).then_inc(ring_read, 1)
                                junk_used[n % 2] = n + 1
                        elif kind == "turned":
                            dve.tensor_copy(ctx_t[:, what * CH:(what + 1) * CH], psum[:, bank, :]).then_inc(ring_read, 1)
                        elif kind == "project":
                            rows = x_res[:, what * BPC:(what + 1) * BPC, :]
                            own(dve.tensor_tensor(rows, rows, bcast_blocks(bo_bc, BPC), ALU.add))
                            own.wait()
                            dve.tensor_tensor(rows, psum[:, bank, :].rearrange("p (b d) -> p b d", d=D), rows,
                                              ALU.add).then_inc(ring_read, 1)
                            dve.wait_ge(ring_read, n + 1)
                        elif kind == "max":
                            k = step_no[what]
                            if k >= 2:
                                dve.wait_ge(negmax_landed[(k - 2) % 4], 16 * MAX_PARTS * ((k - 2) // 4 + 1))
                            src = psum[0:G * BPC, bank, 0:P]
                            own(dve.tensor_scalar(nm_parts[:, k % 2, 0, :], src, 1.0 / MAX_UNIT, None, ALU.mult))
                            own.wait()
                            dve.scalar_tensor_tensor(out=nm_parts[:, k % 2, 1, :], in0=src, scalar=1.0 / MAX_UNIT,
                                                     in1=nm_parts[:, k % 2, 0, :], op0=ALU.mult,
                                                     op1=ALU.subtract).then_inc(ring_read, 1)
                            dve.wait_ge(ring_read, n + 1)
                        else:
                            (g, c), k = what, step_no[what]
                            rows = psum[:, bank, :].rearrange("p (b h w) -> p b h w", h=G, w=VW)
                            own(dve.reciprocal(recip[:, k % 2, :, :], rows[:, :, :, DH]))
                            own.wait()
                            r = recip[:, k % 2, :, :].rearrange("p b (h a) -> p b h a", a=1)
                            dst = ctx[:, c * BPC:(c + 1) * BPC, g * G * DH:(g + 1) * G * DH]
                            dve.tensor_tensor(dst.rearrange("p b (h d) -> p b h d", d=DH), rows[:, :, :, 0:DH],
                                              r.broadcast_to([P, BPC, G, DH]), ALU.mult).then_inc(ring_read, 1)
                            dve.wait_ge(ring_read, n + 1)
                            if g == NG - 1 and not projected:
                                rows = slice(c * BPC, (c + 1) * BPC)
                                own(dve.tensor_tensor(x_res[:, rows, :], ctx[:, rows, :], x_res[:, rows, :], ALU.add))
                    if turn in norm_turn:
                        next_norms.make(dve, own, s1, norm_turn[turn])
                    for s in m_now:
                        k = step_no[s]
                        dve.wait_ge(ring_read, last_unit[s] + 1)
                        if k >= 2:
                            dve.wait_ge(ring_full, ring_no["max", STEPS[k - 2]] + 1)
                        dve.tensor_reduce(neg_max[:, k % 2, :],
                                          part_max[:, k % 2, :, :, 0:s[1] + 1].rearrange("p h i c -> p (h i) c"),
                                          axis=AX.X, op=ALU.max, negate=True).then_inc(negmax_ready, 1)

            @blk.gpsimd
            def _(pool):
                for n in range(1, NCH):
                    pool.wait_ge(parts_stored[n % 2], 16 * 2 * TERMS * (n // 2 + 1))
                    for h in range(G):
                        load_k_rows(pool, proj.order[n], h).then_inc(k_landed[proj.order[n] - 1], 16)

            @blk.sync
            def _(sp):
                def slots_of(n):
                    c = proj.order[n]
                    cols = slice(c * CH, (c + 1) * CH)
                    if n >= 2:
                        sp.wait_ge(parts_stored[n % 2], 16 * 2 * TERMS * (n // 2))
                    for m in range(2):
                        sp.wait_ge(proj.lo_ready, 2 * n + m + 1)
                        for i, r in enumerate((Q_PARTS, K_PARTS)[m]):
                            sp.dma_start(slot_dram[m][:, i, :, cols],
                                         proj.parts_of(n, m)[:, r, :]).then_inc(parts_stored[n % 2], 16)
                    sp.wait_ge(parts_stored[n % 2], 16 * 2 * TERMS * (n // 2 + 1))
                    sp.dma_start(q_slots[:, :, cols],
                                 slot_dram[0].rearrange("(g h) i d t -> (h i d) g t", h=G)[:, :, cols]
                                 ).then_inc(q_landed[c], 16)
                    if n == 0:
                        for h in range(G):
                            load_k_rows(sp, c, h).then_inc(q_landed[c], 16)

                for n in range(NCH - 1):
                    slots_of(n)
                for k, (g, c) in enumerate(STEPS):
                    if k == AHEAD:
                        slots_of(NCH - 1)
                    sp.wait_ge(ring_read, ring_no["max", STEPS[k]] + 1)
                    for r in range(MAX_PARTS):
                        sp.dma_start(q_slots[MAX_ROW + r::SLOT, g, c * CH:(c + 1) * CH],
                                     nm_parts[:, k % 2, r, :]).then_inc(negmax_landed[k % 4], 16)
                for i in range(4):
                    sp.wait_ge(negmax_landed[i], 16 * MAX_PARTS * len(STEPS[i::4]))

            return ring_read, len(ring_no)

        UP, DOWN = (0, 1, 2, 3), (3, 2, 1, 0)
        BETWEEN, TURNING = (3, 2, 0, 1), (0, 3, 1, 2)
        orders = (UP, UP, BETWEEN, TURNING, TURNING, DOWN)
        norms = [Norms(f"xn_ready{i}", order) for i, order in enumerate((UP, UP, BETWEEN, BETWEEN, TURNING, DOWN))]
        projections = {1: Projection(w_qkv0, False, norms[1], orders[1]), 4: Projection(w_qkv1, True, norms[4], orders[4])}
        released = expert_layer(True, orders[0], 0, norms[0], norms[1], following=projections[1])
        released = attention_layer(projections[1], 0, True, 3, norms[2], 2, released)
        released = expert_layer(False, orders[2], 2, norms[2], norms[3], released)
        released = ternary_layer(False, orders[3], 3, norms[3], norms[4], released, projections[4])
        released = attention_layer(projections[4], 1, False, 3, norms[5], 2, released)
        ternary_layer(True, orders[5], 2, norms[5], None, released)


_INS = ['L0_attn_x', 'L0_attn_wq', 'L0_attn_wk', 'L0_attn_wv', 'L0_attn_wo', 'L0_attn_bo', 'L0_ffn_Wr', 'L0_ffn_W1',
        'L0_ffn_b1', 'L0_ffn_Wo', 'L0_ffn_bo', 'L0_ffn_gamma', 'L0_ffn_beta', 'L1_attn_W', 'L1_attn_b', 'L1_ffn_W1',
        'L1_ffn_b1', 'L1_ffn_W2', 'L1_ffn_b2']
_OUT_SHAPE = (1, T, D)


def kernel(**inputs):
    import numpy as _np
    import concourse.bacc as _bacc
    from concourse import mybir as _mybir
    from concourse.bass_utils import run_bass_kernel_spmd as _run

    nc = _bacc.Bacc("TRN2", target_bir_lowering=False, num_devices=1)
    arrays, args = {}, []
    for name in _INS:
        a = _np.ascontiguousarray(inputs[name])
        arrays[f"in_{name}_dram"] = a
        args.append(nc.dram_tensor(f"in_{name}_dram", a.shape, _mybir.dt.from_np(a.dtype), kind="ExternalInput").ap())
    out = nc.dram_tensor("out_0_dram", _OUT_SHAPE, _mybir.dt.float32, kind="ExternalOutput").ap()
    macaron_layers(nc, *args, out)
    r = _run(nc, [arrays], core_ids=[0])
    return r.results[0]["out_0_dram"]
```
